# Optimizing a Trainium2 kernel written in Bass

```python
import numpy as np
import jax
import jax.numpy as jnp

def _softmax(x, axis=-1):
    return jax.nn.softmax(x, axis=axis)

def _gelu(x):
    return jax.nn.gelu(x, approximate=True)

def _silu(x):
    return jax.nn.silu(x)

def _sigmoid(x):
    return jax.nn.sigmoid(x)

def _layernorm(x, axis=-1, eps=1e-05):
    m = jnp.mean(x, axis=axis, keepdims=True)
    v = jnp.var(x, axis=axis, keepdims=True)
    return (x - m) / jnp.sqrt(v + eps)

def _scatter_add(tgt, idx, src, axis=0):
    return tgt.at[idx].add(src)

def _segment_sum(src, seg, n):
    return jax.ops.segment_sum(src, seg, n)
kernel_name = 'mk_seq_postln_d1_jaxref_r8_513749'

def setup_inputs(seed: int=0):
    np.random.seed(seed)
    _w = jnp.asarray

    def _L0_attn_setup():
        import jax, jax.numpy as jnp
        import numpy as np
        import math
        FEATURE_DIM = 128
        NUM_HEADS = 16
        HEAD_SIZE = FEATURE_DIM // NUM_HEADS
        key = jax.random.key(seed)
        ks = jax.random.split(key, 5)
        B, T, C = (4, 256, FEATURE_DIM)
        scale = 1.0 / math.sqrt(C)
        x = jax.random.normal(ks[0], (B, T, C), dtype=jnp.float32)
        W_qkv = jax.random.uniform(ks[1], (3 * C, C), jnp.float32, -scale, scale)
        b_qkv = jax.random.uniform(ks[2], (3 * C,), jnp.float32, -scale, scale)
        W_out = jax.random.uniform(ks[3], (C, C), jnp.float32, -scale, scale)
        b_out = jax.random.uniform(ks[4], (C,), jnp.float32, -scale, scale)
        return {'x': x, 'W_qkv': W_qkv, 'b_qkv': b_qkv, 'W_out': W_out, 'b_out': b_out}
    _L0_attn_in = _L0_attn_setup()

    def _L0_ffn_setup():
        import jax, jax.numpy as jnp
        import numpy as np
        NUM_EXPERTS = 8
        TOP_K = 2
        ROUTE_SCALE = 1.0
        DIM = 128
        HID = 128
        B, S = (2, 512)
        key = jax.random.key(seed)
        ks = jax.random.split(key, 9)
        sc = 0.05
        return {'x': jax.random.normal(ks[0], (B, S, DIM), dtype=jnp.float32), 'gate_w': jax.random.normal(ks[1], (NUM_EXPERTS, DIM), dtype=jnp.float32) * sc, 'w1': jax.random.normal(ks[2], (NUM_EXPERTS, HID, DIM), dtype=jnp.float32) * sc, 'w2': jax.random.normal(ks[3], (NUM_EXPERTS, DIM, HID), dtype=jnp.float32) * sc, 'w3': jax.random.normal(ks[4], (NUM_EXPERTS, HID, DIM), dtype=jnp.float32) * sc, 'sw1': jax.random.normal(ks[5], (HID, DIM), dtype=jnp.float32) * sc, 'sw2': jax.random.normal(ks[6], (DIM, HID), dtype=jnp.float32) * sc, 'sw3': jax.random.normal(ks[7], (HID, DIM), dtype=jnp.float32) * sc, 'expert_bias': jnp.zeros((NUM_EXPERTS,), dtype=jnp.float32)}
    _L0_ffn_in = _L0_ffn_setup()
    _d = {'L0_attn_x': _L0_attn_in['x'], 'L0_attn_W_qkv': _L0_attn_in['W_qkv'], 'L0_attn_b_qkv': _L0_attn_in['b_qkv'], 'L0_attn_W_out': _L0_attn_in['W_out'], 'L0_attn_b_out': _L0_attn_in['b_out'], 'L0_ffn_gate_w': _L0_ffn_in['gate_w'], 'L0_ffn_w1': _L0_ffn_in['w1'], 'L0_ffn_w2': _L0_ffn_in['w2'], 'L0_ffn_w3': _L0_ffn_in['w3'], 'L0_ffn_sw1': _L0_ffn_in['sw1'], 'L0_ffn_sw2': _L0_ffn_in['sw2'], 'L0_ffn_sw3': _L0_ffn_in['sw3'], 'L0_ffn_expert_bias': _L0_ffn_in['expert_bias']}
    _x0 = _d['L0_attn_x']
    _d['L0_attn_x'] = jax.random.normal(jax.random.fold_in(jax.random.key(seed), 1), (32, 256, 128), dtype=_x0.dtype)
    del _x0
    return _d

def reference(L0_attn_x, L0_attn_W_qkv, L0_attn_b_qkv, L0_attn_W_out, L0_attn_b_out, L0_ffn_gate_w, L0_ffn_w1, L0_ffn_w2, L0_ffn_w3, L0_ffn_sw1, L0_ffn_sw2, L0_ffn_sw3, L0_ffn_expert_bias):

    def _L0_attn_ref(x, W_qkv, b_qkv, W_out, b_out):
        import jax, jax.numpy as jnp
        import numpy as np
        import math
        FEATURE_DIM = 128
        NUM_HEADS = 16
        HEAD_SIZE = FEATURE_DIM // NUM_HEADS
        B, T, C = x.shape
        H, hs = (NUM_HEADS, HEAD_SIZE)
        qkv = x @ W_qkv.T + b_qkv
        qkv = qkv.reshape(B, T, H, 3 * hs)
        q = qkv[..., :hs]
        k = qkv[..., hs:2 * hs]
        v = qkv[..., 2 * hs:]
        att = jnp.einsum('bthd,bshd->bhts', q, k) / math.sqrt(hs)
        att_prob = jax.nn.softmax(att, axis=-1)
        att_v = jnp.einsum('bhts,bshd->bthd', att_prob, v)
        att_v = att_v.reshape(B, T, C)
        return att_v @ W_out.T + b_out

    def _L0_ffn_ref(x, gate_w, w1, w2, w3, sw1, sw2, sw3, expert_bias):
        import jax, jax.numpy as jnp
        import numpy as np
        NUM_EXPERTS = 8
        TOP_K = 2
        ROUTE_SCALE = 1.0
        DIM = 128
        HID = 128
        B, S = (2, 512)
        bs, slen, dim = x.shape
        xf = x.reshape(-1, dim)
        scores = jax.nn.sigmoid((xf @ gate_w.T).astype(jnp.float32))
        _, sel = jax.lax.top_k(scores + expert_bias[None, :], TOP_K)
        top_scores = jnp.take_along_axis(scores, sel, axis=1) * ROUTE_SCALE
        flat_sel = sel.reshape(-1)
        order = jnp.argsort(flat_sel, stable=True)
        scores_sorted = top_scores.reshape(-1)[order]
        tok_idx = order // TOP_K
        expert_ids = flat_sel[order]
        routed = xf[tok_idx]
        routed = (routed.astype(jnp.float32) * scores_sorted[:, None]).astype(x.dtype)
        out_r = jnp.zeros_like(routed)
        for e in range(NUM_EXPERTS):
            m = (expert_ids == e)[:, None]
            h = jax.nn.silu(routed @ w1[e].T) * (routed @ w3[e].T)
            out_r = out_r + jnp.where(m, h @ w2[e].T, jnp.zeros((), routed.dtype))
        shared = jax.nn.silu(xf @ sw1.T) * (xf @ sw3.T) @ sw2.T
        out_r = (out_r.astype(jnp.float32) * scores_sorted[:, None]).astype(x.dtype)
        out = shared.at[tok_idx].add(out_r)
        return out.reshape(bs, slen, dim)
    x = L0_attn_x
    x = _layernorm(x + _L0_attn_ref(x, L0_attn_W_qkv, L0_attn_b_qkv, L0_attn_W_out, L0_attn_b_out), axis=-1)
    x = _layernorm(x + _L0_ffn_ref(x, L0_ffn_gate_w, L0_ffn_w1, L0_ffn_w2, L0_ffn_w3, L0_ffn_sw1, L0_ffn_sw2, L0_ffn_sw3, L0_ffn_expert_bias), axis=-1)
    return x

_drawn_inputs = setup_inputs


def setup_inputs(seed=0):
    import zlib

    import numpy as np

    out = dict(_drawn_inputs(seed))
    spreads = {'L0_ffn_expert_bias': (0.0, 0.31)}
    factors = {'L0_ffn_gate_w': 2.791}
    for name, (base, spread) in spreads.items():
        noise = np.random.default_rng([zlib.crc32(name.encode()), seed]).standard_normal(out[name].shape)
        drawn = base * np.exp(spread * noise) if base else spread * noise
        out[name] = jnp.asarray(drawn.astype(out[name].dtype))
    for name, factor in factors.items():
        out[name] = (out[name] * factor).astype(out[name].dtype)
    return out
```

```python
from contextlib import ExitStack

import numpy as np

import concourse.bass as bass
from concourse import mybir

ALU = mybir.AluOpType
ACT = mybir.ActivationFunctionType
AX_X = mybir.AxisListType.X
F32 = mybir.dt.float32
BF16 = mybir.dt.bfloat16

P = 128
RING = 4
PARTS = 3
QPART = (0, 0, 0, 1, 1, 2)
KPART = (0, 1, 2, 0, 1, 0)
TWO_ONES = float(np.array([0x3F803F80], np.uint32).view(np.float32)[0])
MAXROW = 96


class Batch:

    def __init__(self, i, c, batches):
        self.i, self.c = i, c
        self.n = i * RING + c
        self.ring = c % RING
        self.looped = not isinstance(i, int)
        self.live = self.looped or 0 <= c < batches

    def later(self, k):
        assert not self.looped or self.c >= k
        return self.c >= k

    def count(self, per, more):
        assert per * self.c + more >= 0
        return self.i * (RING * per) + (per * self.c + more)

    def lap(self, per, more):
        return self.i * per + (per * (self.c // RING) + more)


def attention_moe_layer(nc, x, xT, wqT, wkT, wvT, bq, bk, bv, woT, bo, gateT, ebias, rank, w1T, w3T, w2T, out):
    C, N = xT.shape
    B = 32
    T = N // B
    NT = T // P
    D = 8
    H = C // D
    E = gateT.shape[1]
    NE = E + 1
    TILES = N // P
    SCALE = float(D) ** -0.5
    EPS = 1e-5
    G = 512
    GT = G // P
    GROUPS = N // G
    NC = len(QPART)
    assert C == P and H == 16 and NT == 2 and NC * D <= MAXROW

    with ExitStack() as ctx:
        def sb(name, shape, dt=F32):
            return ctx.enter_context(nc.sbuf_tensor(name, shape, dt))

        def sem(name):
            return ctx.enter_context(nc.semaphore(name))

        q_parts_dram = nc.dram_tensor("q_parts_dram", [RING, H, NC, D, T], BF16, kind="Internal").ap()
        k_parts_dram = nc.dram_tensor("k_parts_dram", [RING, H, PARTS, D, T], BF16, kind="Internal").ap()
        route_dram = nc.dram_tensor("route_dram", [TILES, E, P], F32, kind="Internal").ap()

        wq_sb, wk_sb, wv_sb, wo_sb = (sb(n, [P, C]) for n in ("wq_sb", "wk_sb", "wv_sb", "wo_sb"))
        bq_sb, bk_sb, bqs = sb("bq_sb", [P, 1]), sb("bk_sb", [P, 1]), sb("bqs", [P, 1])
        bv_sb = sb("bv_sb", [P, NT, C])
        bo_sb = sb("bo_sb", [P, C])
        gate_sb = sb("gate_sb", [P, E])
        ebias_sb, rank_sb = sb("ebias_sb", [P, E]), sb("rank_sb", [P, E])
        w1_sb, w3_sb, w2_sb = (sb(n, [P, NE, P]) for n in ("w1_sb", "w3_sb", "w2_sb"))
        ident = sb("ident", [P, P])
        minus_half = sb("minus_half", [P, GT])
        x1 = sb("x1", [P, TILES, C])
        x1T = sb("x1T", [P, N])
        logits = sb("logits", [P, TILES, E])

        xT_sb = [sb(f"xT_sb{r}", [P, T]) for r in range(RING)]
        x_sb = [sb(f"x_sb{r}", [P, NT, C]) for r in range(RING)]
        q_stack = [sb(f"q_stack{r}", [P, H, T], BF16) for r in range(RING)]
        k_stack = [sb(f"k_stack{r}", [P, H, T], BF16) for r in range(RING)]
        v_aug = [sb(f"v_aug{r}", [P, 2 * NT, 2, 4, 32]) for r in range(RING)]
        negmax = [sb(f"negmax{r}", [P, NT, H]) for r in range(2)]
        qf, kf, rq, rk = (sb(n, [P, T]) for n in ("qf", "kf", "rq", "rk"))
        q_parts, k_parts = sb("q_parts", [P, PARTS, T], BF16), sb("k_parts", [P, PARTS, T], BF16)
        max_hi, max_lo = sb("max_hi", [H, T], BF16), sb("max_lo", [H, T], BF16)
        probs = [sb(f"probs{r}", [P, NT, T]) for r in range(8)]
        attT = sb("attT", [P, 2, T])
        recip_sum = sb("recip_sum", [P, 8 * NT, 2])
        att_tok = sb("att_tok", [P, 8 * NT, 2, D])
        attc = sb("attc", [P, T])
        x_bo = sb("x_bo", [P, NT, C])
        res = sb("res", [P, NT, C])
        stats, mv = sb("stats", [P, NT, 6]), sb("mv", [P, NT, 2])
        var_eps, rstd = sb("var_eps", [P, NT]), sb("rstd", [P, NT])
        x1_new, x1T_new = sb("x1_new", [P, NT, C]), sb("x1T_new", [P, T])

        banks = [ctx.enter_context(nc.psum_tensor(f"bank{n}", [P, 512], F32)) for n in range(8)]
        max_ps, score_ps, av_ps = banks[0:2], banks[2:4], banks[4:6]
        misc_act, misc_dve = banks[6], banks[7]

        w_in, xT_in, x_in = sem("w_in"), [sem(f"xT_in{r}") for r in range(RING)], [sem(f"x_in{r}") for r in range(RING)]
        c_in = sem("c_in")
        q_clear, k_clear, v_clear, consts_set = sem("q_clear"), sem("k_clear"), sem("v_clear"), sem("consts_set")
        bqs_set = sem("bqs_set")
        qk_mm, v_mm = sem("qk_mm"), sem("v_mm")
        qk_f = sem("qk_f")
        split_step, parts_out = sem("split_step"), sem("parts_out")
        stack_in = [sem(f"stack_in{r}") for r in range(RING)]
        max_in = [sem(f"max_in{r}") for r in range(RING)]
        v_set = sem("v_set")
        max_mm, max_red = sem("max_mm"), sem("max_red")
        max_T, max_hi_set, max_split = sem("max_T"), sem("max_hi_set"), sem("max_split")
        score_mm, exp_done = sem("score_mm"), sem("exp_done")
        av_mm, att_sb = sem("av_mm"), sem("att_sb")
        tok_T, recip_set, att_norm = sem("tok_T"), sem("recip_set"), sem("att_norm")
        back_T, attc_set = sem("back_T"), sem("attc_set")
        y_mm, xbo_set, res_set = sem("y_mm"), sem("xbo_set"), sem("res_set")
        stats_set, mv_set, eps_set, rstd_set = sem("stats_set"), sem("mv_set"), sem("eps_set"), sem("rstd_set")
        x1_set, x1_kept, x1_T, x1T_set, x1T_kept = (sem(n) for n in ("x1_set", "x1_kept", "x1_T", "x1T_set", "x1T_kept"))
        gate_mm, logits_set = sem("gate_mm"), sem("logits_set")

        class Slot:
            def __init__(self, i, s):
                self.proj, self.maxi, self.neg, self.soft, self.tail = (
                    Batch(i, s + k, B) for k in (3, 2, 1, 0, -1))

        FIRST, LOOPS = 2, (B - 8) // RING

        def slots(engine, body):
            for s in range(-3, FIRST):
                body(Slot(0, s))
            with engine.Fori(0, LOOPS) as i:
                for s in range(FIRST, FIRST + RING):
                    body(Slot(i, s))
            for s in range(FIRST + RING * LOOPS, B + 1):
                body(Slot(0, s))

        DEPTH = 3
        SB_RING = 4
        places = [stack[:].rearrange("p h t -> p (h t)").bitcast(F32)[:, n * G:(n + 1) * G]
                  for stack in q_stack + k_stack for n in range(H * T // 2 // G)]

        def take(count):
            return [places.pop(0) for _ in range(count)]

        xs, act, hid, hid_s = (take(DEPTH) for _ in range(4))
        weight_b = take(SB_RING)
        by_tile = [v.rearrange("p (a e) -> p a e", e=E) for v in take(5)]
        scores, biased, equal, weights, first_sel = by_tile
        weightsT, outT, y_sb, res2 = take(4)
        weightsT, y_sb, res2 = (v.rearrange("p (a c) -> p a c", c=P) for v in (weightsT, y_sb, res2))
        best = sb("best", [P, TILES])
        stats2, mv2 = sb("stats2", [P, GT, 6]), sb("mv2", [P, GT, 2])
        var_eps2, rstd2 = sb("var_eps2", [P, GT]), sb("rstd2", [P, GT])
        up1_ps, up3_ps, down_ps, outT_ps = banks[0:3], banks[3:6], banks[6], banks[7]
        scores_set, route_step, weights_T, weightsT_set, route_out = (
            sem(n) for n in ("scores_set", "route_step", "weights_T", "weightsT_set", "route_out"))
        weight_in = [sem(f"weight_in{r}") for r in range(SB_RING)]
        xs_set, up_mm, act_set, hid_set, hids_set, down_mm = (
            sem(n) for n in ("xs_set", "up_mm", "act_set", "hid_set", "hids_set", "down_mm"))
        outT_set, out_T, res2_set, stats2_set, mv2_set, eps2_set, rstd2_set, y_set, y_out = (
            sem(n) for n in ("outT_set", "out_T", "res2_set", "stats2_set", "mv2_set", "eps2_set", "rstd2_set",
                             "y_set", "y_out"))

        def groups(engine, body):
            body(0)
            body(1)
            with engine.Fori(0, GROUPS - 2) as i:
                body(i + 2)

        def past(g, n):
            return not isinstance(g, int) or g >= n

        block = ctx.enter_context(nc.Block())

        @block.sync
        def _(sp):
            for dst, src in ((wv_sb, wvT), (wq_sb, wqT), (wk_sb, wkT), (bq_sb, bq), (bk_sb, bk),
                             (bv_sb, bv.to_broadcast([P, NT, C]))):
                sp.dma_start(dst[:], src).then_inc(w_in, 16)

            def slot(t):
                b, m = t.proj, t.neg
                if b.live:
                    if b.later(RING):
                        sp.wait_ge(v_mm, b.count(1, 1 - RING))
                        sp.wait_ge(qk_mm, b.count(1, 1 - RING))
                    sp.dma_start(xT_sb[b.ring][:], xT[:, bass.ds(b.n * T, T)]).then_inc(xT_in[b.ring], 16)
                if m.live:
                    sp.wait_ge(max_split, m.count(1, 1))
                    for row, part in enumerate((max_hi, max_lo)):
                        sp.dma_start(q_stack[m.ring][MAXROW + row:MAXROW + row + 1, :, :], part[:]).then_inc(max_in[m.ring], 16)
                if b.live:
                    if b.later(RING):
                        sp.wait_ge(score_mm, b.count(H, H * (1 - RING)))
                        sp.wait_ge(xbo_set, b.count(1, 1 - RING))
                    else:
                        sp.wait_ge(q_clear, b.c + 1)
                        sp.wait_ge(k_clear, 2 * (b.c + 1))
                    sp.dma_start(x_sb[b.ring][:], x[bass.ds(b.n * NT, NT), :, :].rearrange("i p c -> p i c")).then_inc(x_in[b.ring], 16)
                    sp.wait_ge(split_step, b.count(6, 6))
                    for c, part in enumerate(QPART):
                        sp.dma_start(q_parts_dram[b.ring, :, c], q_parts[:, part, :]).then_inc(parts_out, 16)
                    for c in range(PARTS):
                        sp.dma_start(k_parts_dram[b.ring, :, c], k_parts[:, c, :]).then_inc(parts_out, 16)
                    sp.wait_ge(parts_out, b.count(144, 144))
                    sp.dma_start(q_stack[b.ring][0:NC * D, :, :], q_parts_dram[b.ring].rearrange("h c d t -> (c d) h t")).then_inc(stack_in[b.ring], 16)
                    for row, parts in ((0, 3), (3, 2), (5, 1)):
                        sp.dma_start(k_stack[b.ring][row * D:(row + parts) * D, :, :],
                                     k_parts_dram[b.ring, :, 0:parts].rearrange("h c d t -> (c d) h t")).then_inc(stack_in[b.ring], 16)

            slots(sp, slot)

            sp.wait_ge(weightsT_set, 1)
            sp.dma_start(route_dram.rearrange("(c r) e t -> (r e) c t", r=16), weightsT[:]).then_inc(route_out, 16)
            sp.wait_ge(route_out, 16)

            def write_out(g):
                sp.wait_ge(y_set, g * GT)
                sp.dma_start(out[bass.ds(g * GT - GT, GT), :, :].rearrange("i p c -> p i c"), y_sb[:]).then_inc(y_out, 16)

            def group(g):
                for e in range(E):
                    if past(g, 1) or e >= SB_RING:
                        sp.wait_ge(hids_set, g * E + (e - SB_RING + 1))
                        sp.wait_ge(xs_set, g * E + (e - SB_RING + 1))
                    sp.dma_start(weight_b[e % SB_RING].rearrange("p (a t) -> p a t", t=P),
                                 route_dram[bass.ds(g * GT, GT), e:e + 1, :].rearrange("a e t -> e a t").to_broadcast([P, GT, P])
                                 ).then_inc(weight_in[e % SB_RING], 16)
                if past(g, 1):
                    write_out(g)

            groups(sp, group)
            write_out(GROUPS)
            sp.wait_ge(y_out, 16 * GROUPS)

        @block.gpsimd
        def _(pool):
            pool.memset(ident[:], 0.0).then_inc(consts_set, 1)
            pool.wait_ge(consts_set, 1)
            pool.affine_select(out=ident[:], in_=ident[:], compare_op=ALU.not_equal, fill=1.0, base=0,
                               pattern=[[-1, P]], channel_multiplier=1).then_inc(consts_set, 1)
            pool.memset(minus_half[:], -0.5).then_inc(consts_set, 1)
            for r in range(RING):
                pool.memset(q_stack[r][:].rearrange("p h t -> p (h t)").bitcast(F32), 0.0).then_inc(q_clear, 1)
            pool.wait_ge(c_in, 16 * 8)

            def slot(t):
                b = t.tail
                if b.live:
                    pool.wait_ge(x_in[b.ring], b.lap(16, 16))
                    pool.wait_ge(res_set, b.count(1, 0))
                    pool.tensor_tensor(x_bo[:], x_sb[b.ring][:], bo_sb[:].unsqueeze(1).to_broadcast([P, NT, C]), ALU.add).then_inc(xbo_set, 1)
                b = t.proj
                if b.live:
                    pool.wait_ge(qk_f, b.count(4, 4))
                    for full, rest, parts in ((qf, rq, q_parts), (kf, rk, k_parts)):
                        pool.tensor_tensor(rest[:], full[:], parts[:, 0, :], ALU.subtract).then_inc(split_step, 1)
                        pool.tensor_tensor(parts[:, 1, :], full[:], parts[:, 0, :], ALU.subtract).then_inc(split_step, 1)
                    pool.wait_ge(split_step, b.count(6, 2))
                    pool.tensor_tensor(q_parts[:, 2, :], rq[:], q_parts[:, 1, :], ALU.subtract).then_inc(split_step, 1)
                    pool.wait_ge(split_step, b.count(6, 4))
                    pool.tensor_tensor(k_parts[:, 2, :], rk[:], k_parts[:, 1, :], ALU.subtract).then_inc(split_step, 1)
                b = t.tail
                if b.live:
                    pool.wait_ge(eps_set, b.count(1, 1))
                    pool.tensor_tensor(rstd[:], var_eps[:], minus_half[:, 0:NT], ALU.pow).then_inc(rstd_set, 1)
                    pool.wait_ge(x1_set, b.count(2, 2))
                    pool.tensor_copy(x1[:, bass.ds(b.n * NT, NT), :], x1_new[:]).then_inc(x1_kept, 1)
                    pool.wait_ge(x1T_set, b.count(1, 1))
                    pool.tensor_copy(x1T[:, bass.ds(b.n * T, T)], x1T_new[:]).then_inc(x1T_kept, 1)

            slots(pool, slot)

            def group(g):
                for e in range(E):
                    n = e + 1
                    if past(g, 1) or n >= DEPTH:
                        pool.wait_ge(down_mm, g * NE + (n - DEPTH + 1))
                    pool.wait_ge(hid_set, g * NE + (n + 1))
                    pool.tensor_tensor(hid_s[n % DEPTH][:], hid[n % DEPTH][:], weight_b[e % SB_RING],
                                       ALU.mult).then_inc(hids_set, 1)
                    if e == 3:
                        if not past(g, 1):
                            continue
                        pool.wait_ge(eps2_set, g)
                        pool.tensor_tensor(rstd2[:], var_eps2[:], minus_half[:], ALU.pow).then_inc(rstd2_set, 1)

            groups(pool, group)
            pool.wait_ge(eps2_set, GROUPS)
            pool.tensor_tensor(rstd2[:], var_eps2[:], minus_half[:], ALU.pow).then_inc(rstd2_set, 1)

        @block.scalar
        def _(act_e):
            for dst, src in ((wo_sb, woT), (bo_sb, bo.to_broadcast([P, C])),
                             (gate_sb, gateT), (ebias_sb, ebias.to_broadcast([P, E])), (rank_sb, rank.to_broadcast([P, E])),
                             (w1_sb, w1T), (w3_sb, w3T), (w2_sb, w2T)):
                act_e.dma_start(dst[:], src).then_inc(c_in, 16)

            def slot(t):
                for h in range(H):
                    b = t.soft
                    if b.live:
                        act_e.wait_ge(score_mm, b.count(H, h + 1))
                        if h % 4 == 0 and b.later(1) or h >= 8 and h % 4 == 0:
                            act_e.wait_ge(av_mm, b.count(4, h // 4 - 1))
                        nc.scalar.activation(probs[h % 8][:], score_ps[h % 2][:].rearrange("p (j t) -> p j t", j=NT), ACT.Exp).then_inc(exp_done, 1)
                    b = t.proj
                    if b.live and h == 3:
                        if b.c == 0 and not b.looped:
                            act_e.wait_ge(bqs_set, 1)
                        act_e.wait_ge(qk_mm, b.count(1, 1))
                        if b.later(1):
                            act_e.wait_ge(split_step, b.count(6, 0))
                            act_e.wait_ge(parts_out, b.count(144, 0))
                        nc.scalar.activation(qf[:], misc_act[:, 0:T], ACT.Identity, bias=bqs[:, 0:1], scale=SCALE).then_inc(qk_f, 1)
                        nc.scalar.activation(q_parts[:, 0, :], misc_act[:, 0:T], ACT.Identity, bias=bqs[:, 0:1], scale=SCALE).then_inc(qk_f, 1)
                    if b.live and h == 4:
                        nc.scalar.activation(kf[:], misc_act[:, T:2 * T], ACT.Identity, bias=bk_sb[:, 0:1]).then_inc(qk_f, 1)
                        nc.scalar.activation(k_parts[:, 0, :], misc_act[:, T:2 * T], ACT.Identity, bias=bk_sb[:, 0:1]).then_inc(qk_f, 1)
                    b = t.tail if h == 4 else t.soft
                    if b.live and h in (4, 12):
                        half = 1 if h == 4 else 0
                        act_e.wait_ge(av_mm, b.count(4, 2 * half + 2))
                        act_e.wait_ge(tok_T, b.count(1, 0))
                        nc.scalar.activation(attT[:, half, :], av_ps[half][:, 0:T], ACT.Copy).then_inc(att_sb, 1)
                    b = t.tail
                    if b.live and h == 10:
                        act_e.wait_ge(back_T, b.count(1, 1))
                        act_e.wait_ge(y_mm, b.count(1, 0))
                        nc.scalar.activation(attc[:], misc_act[:, 0:T], ACT.Copy).then_inc(attc_set, 1)
                    if b.live and h == 15:
                        act_e.wait_ge(x1_T, b.count(1, 1))
                        act_e.wait_ge(gate_mm, b.count(1, 0))
                        act_e.wait_ge(x1T_kept, b.count(1, 0))
                        nc.scalar.activation(x1T_new[:], misc_act[:, T:2 * T], ACT.Copy).then_inc(x1T_set, 1)

            slots(act_e, slot)

            act_e.wait_ge(logits_set, B)
            nc.scalar.activation(scores[:], logits[:], ACT.Sigmoid).then_inc(scores_set, 1)

            def drain(g):
                act_e.wait_ge(down_mm, g * NE)
                if past(g, 2):
                    act_e.wait_ge(out_T, g - 1)
                nc.scalar.activation(outT[:], down_ps[:], ACT.Copy).then_inc(outT_set, 1)

            def group(g):
                for n in range(NE):
                    act_e.wait_ge(up_mm, g * (2 * NE) + (2 * n + 1))
                    if past(g, 1) or n >= DEPTH:
                        act_e.wait_ge(hid_set, g * NE + (n - DEPTH + 1))
                    nc.scalar.activation(act[n % DEPTH][:], up1_ps[n % DEPTH][:], ACT.Silu).then_inc(act_set, 1)
                    if n == 0 and past(g, 1):
                        drain(g)

            groups(act_e, group)
            drain(GROUPS)

        @block.tensor
        def _(pe):
            def row_maxima_scores(b, h):
                if h == 0:
                    pe.wait_ge(stack_in[b.ring], b.lap(64, 64))
                if b.later(1) or h >= 2:
                    pe.wait_ge(max_red, b.count(H, h - 1))
                for i in range(NT):
                    mm = pe.matmul(max_ps[h % 2][:, i * T:(i + 1) * T], q_stack[b.ring][0:MAXROW, h, i * P:(i + 1) * P],
                                   k_stack[b.ring][0:MAXROW, h, :], start=True, stop=True)
                mm.then_inc(max_mm, 1)

            def shifted_scores(b, h):
                if h == 0:
                    pe.wait_ge(max_in[b.ring], b.lap(32, 32))
                    if b.c == 0 and not b.looped:
                        pe.wait_ge(c_in, 16 * 8)
                if b.later(1) or h >= 2:
                    pe.wait_ge(exp_done, b.count(H, h - 1))
                for j in range(NT):
                    mm = pe.matmul(score_ps[h % 2][:, j * T:(j + 1) * T], k_stack[b.ring][:, h, j * P:(j + 1) * P],
                                   q_stack[b.ring][:, h, :], start=True, stop=True)
                mm.then_inc(score_mm, 1)

            def values(b, quad):
                half, u = quad // 2, quad % 2
                pe.wait_ge(exp_done, b.count(H, 4 * quad + 4))
                if u == 0:
                    pe.wait_ge(v_set, b.count(2, 2))
                    if b.later(1):
                        pe.wait_ge(att_sb, b.count(2, half - 1))
                for j in range(NT):
                    for hh in range(4):
                        mm = pe.matmul(av_ps[half][32 * hh:32 * hh + 32, 0:T], v_aug[b.ring][:, 2 * j + half, u, hh, :],
                                       probs[4 * (quad % 2) + hh][:, j, :], start=(u == 0 and j == 0), stop=(u == 1 and j == 1))
                mm.then_inc(av_mm, 1)

            def slot(t):
                for h in range(H):
                    if t.maxi.live:
                        row_maxima_scores(t.maxi, h)
                    if t.soft.live:
                        shifted_scores(t.soft, h)
                    b = t.neg
                    if b.live and h == 1:
                        pe.wait_ge(max_red, b.count(H, H))
                        if t.tail.live and t.tail.later(0):
                            pe.wait_ge(logits_set, t.tail.count(1, 0))
                        if b.c == 0 and not b.looped:
                            pe.wait_ge(consts_set, 3)
                        for i in range(NT):
                            mm = pe.transpose(misc_dve[0:H, T + i * P:T + (i + 1) * P], negmax[b.ring % 2][:, i, :], ident[:])
                        mm.then_inc(max_T, 1)
                    b = t.proj
                    if b.live and h == 3:
                        if b.c == 0 and not b.looped:
                            pe.wait_ge(w_in, 16 * 6)
                        pe.wait_ge(xT_in[b.ring], b.lap(16, 16))
                        if t.tail.live:
                            pe.wait_ge(res_set, t.tail.count(1, 0))
                        if b.later(1):
                            pe.wait_ge(v_set, b.count(2, 0))
                        if t.neg.live:
                            pe.wait_ge(max_split, t.neg.count(1, 1))
                        for i in range(NT):
                            mm = pe.matmul(misc_dve[:, i * P:(i + 1) * P], xT_sb[b.ring][:, i * P:(i + 1) * P], wv_sb[:], start=True, stop=True)
                        mm.then_inc(v_mm, 1)
                    if b.live and h == 3:
                        if b.later(1):
                            pe.wait_ge(qk_f, b.count(4, 0))
                        if t.tail.live:
                            pe.wait_ge(attc_set, t.tail.count(1, 0))
                            pe.wait_ge(x1T_set, t.tail.count(1, 0))
                        pe.matmul(misc_act[:, 0:T], wq_sb[:], xT_sb[b.ring][:], start=True, stop=True)
                        pe.matmul(misc_act[:, T:2 * T], wk_sb[:], xT_sb[b.ring][:], start=True, stop=True).then_inc(qk_mm, 1)
                    if t.tail.live and h == 3:
                        values(t.tail, 3)
                    if t.soft.live and h in (7, 11, 15):
                        values(t.soft, h // 4 - 1)
                    b = t.tail
                    if b.live and h == 6:
                        pe.wait_ge(att_sb, b.count(2, 2))
                        if t.neg.live:
                            pe.wait_ge(max_split, t.neg.count(1, 1))
                        if t.proj.live:
                            pe.wait_ge(v_set, t.proj.count(2, 2))
                        pe.wait_ge(res_set, b.count(1, 0))
                        pe.wait_ge(logits_set, b.count(1, 0))
                        for i in range(NT):
                            for half in range(2):
                                mm = pe.transpose(misc_dve[:, (2 * i + half) * P:(2 * i + half + 1) * P],
                                                  attT[:, half, i * P:(i + 1) * P], ident[:])
                        mm.then_inc(tok_T, 1)
                    if b.live and h == 9:
                        pe.wait_ge(att_norm, b.count(1, 1))
                        if t.proj.live:
                            pe.wait_ge(qk_f, t.proj.count(4, 4))
                        pe.wait_ge(attc_set, b.count(1, 0))
                        for i in range(NT):
                            mm = pe.transpose(misc_act[:, i * P:(i + 1) * P],
                                              att_tok[:, 8 * i:8 * i + 8].rearrange("p a u d -> p (a u d)"), ident[:])
                        mm.then_inc(back_T, 1)
                    if b.live and h == 11:
                        pe.wait_ge(attc_set, b.count(1, 1))
                        pe.wait_ge(att_norm, b.count(1, 1))
                        for i in range(NT):
                            mm = pe.matmul(misc_dve[:, i * P:(i + 1) * P], attc[:, i * P:(i + 1) * P], wo_sb[:], start=True, stop=True)
                        mm.then_inc(y_mm, 1)
                    if b.live and h == 14:
                        pe.wait_ge(x1_set, b.count(2, 2))
                        pe.wait_ge(attc_set, b.count(1, 1))
                        pe.wait_ge(x1T_set, b.count(1, 0))
                        for i in range(NT):
                            mm = pe.transpose(misc_act[:, T + i * P:T + (i + 1) * P], x1_new[:, i, :], ident[:])
                        mm.then_inc(x1_T, 1)
                    if b.live and h == 15:
                        pe.wait_ge(res_set, b.count(1, 1))
                        pe.wait_ge(x1T_set, b.count(1, 1))
                        for i in range(NT):
                            mm = pe.matmul(misc_dve[:, T + i * E:T + (i + 1) * E], x1T_new[:, i * P:(i + 1) * P], gate_sb[:], start=True, stop=True)
                        mm.then_inc(gate_mm, 1)

            slots(pe, slot)

            pe.wait_ge(route_step, 14)
            pe.wait_ge(logits_set, B)
            for c in range(TILES // 16):
                mm = pe.transpose(outT_ps[:, c * P:(c + 1) * P], weights[:, 16 * c:16 * c + 16, :].rearrange("p a e -> p (a e)"), ident[:])
            mm.then_inc(weights_T, 1)
            pe.wait_ge(max_red, H * B)
            pe.wait_ge(exp_done, H * B)
            pe.wait_ge(att_sb, 2 * B)
            pe.wait_ge(x1T_set, B)
            pe.wait_ge(x1T_kept, B)
            pe.wait_ge(weightsT_set, 1)

            def up(g, n):
                if past(g, 1) or n >= DEPTH:
                    pe.wait_ge(act_set, g * NE + (n - DEPTH + 1))
                    pe.wait_ge(hid_set, g * NE + (n - DEPTH + 1))
                if n:
                    pe.wait_ge(xs_set, g * E + n)
                rhs = xs[n % DEPTH][:] if n else x1T[:, bass.ds(g * G, G)]
                pe.matmul(up1_ps[n % DEPTH][:], w1_sb[:, n, :], rhs, start=True, stop=True).then_inc(up_mm, 1)
                pe.matmul(up3_ps[n % DEPTH][:], w3_sb[:, n, :], rhs, start=True, stop=True).then_inc(up_mm, 1)

            def down(g, n):
                if n == 0:
                    pe.wait_ge(hid_set, g * NE + 1)
                    if past(g, 1):
                        pe.wait_ge(outT_set, g)
                    rhs = hid[0][:]
                else:
                    pe.wait_ge(hids_set, g * E + n)
                    rhs = hid_s[n % DEPTH][:]
                pe.matmul(down_ps[:], w2_sb[:, n, :], rhs, start=(n == 0), stop=(n == NE - 1)).then_inc(down_mm, 1)

            def by_tokens(g):
                pe.wait_ge(outT_set, g)
                if past(g, 2):
                    pe.wait_ge(res2_set, g - 1)
                for i in range(GT):
                    mm = pe.transpose(outT_ps[:, i * P:(i + 1) * P], outT[:, i * P:(i + 1) * P], ident[:])
                mm.then_inc(out_T, 1)

            def group(g):
                for n in range(NE):
                    up(g, n)
                    if n:
                        down(g, n - 1)
                    elif past(g, 1):
                        down(g - 1, NE - 1)
                    if n == 2 and past(g, 1):
                        by_tokens(g)

            groups(pe, group)
            down(GROUPS - 1, NE - 1)
            by_tokens(GROUPS)

        @block.vector
        def _(dve):
            for r in range(RING):
                flat = k_stack[r][:].rearrange("p h t -> p (h t)").bitcast(F32)
                dve.memset(flat, 0.0).then_inc(k_clear, 1)
                dve.wait_ge(k_clear, 2 * r + 1)
                dve.memset(flat[MAXROW:P, :], TWO_ONES).then_inc(k_clear, 1)
                dve.memset(v_aug[r][:], 0.0).then_inc(v_clear, 1)
                dve.wait_ge(v_clear, 2 * r + 1)
                for u in range(2):
                    ins = dve.memset(v_aug[r][:, :, u, :, 2 * D + u:2 * D + u + 1], 1.0)
                ins.then_inc(v_clear, 1)
            dve.wait_ge(w_in, 16 * 6)
            dve.tensor_scalar(bqs[:], bq_sb[:], SCALE, None, ALU.mult).then_inc(bqs_set, 1)
            dve.wait_ge(v_clear, 2 * RING)

            def slot(t):
                for h in range(H):
                    if t.tail.live and h == 12:
                        dve.wait_ge(stats_set, t.tail.count(NT, NT))
                    b = t.maxi
                    if b.live:
                        dve.wait_ge(max_mm, b.count(H, h + 1))
                        if h == 0 and b.later(2):
                            dve.wait_ge(max_T, b.count(1, -1))
                        nc.vector.tensor_reduce(negmax[b.ring % 2][:, :, h], max_ps[h % 2][:].rearrange("p (i s) -> p i s", i=NT),
                                                AX_X, ALU.max, negate=True).then_inc(max_red, 1)
                    b = t.neg
                    if b.live and h == 1:
                        dve.wait_ge(max_T, b.count(1, 1))
                        if b.later(1):
                            prev = (b.ring - 1) % RING
                            dve.wait_ge(max_in[prev], Batch(b.i, b.c - 1, B).lap(32, 32))
                        nc.vector.tensor_copy(max_hi[:], misc_dve[0:H, T:2 * T]).then_inc(max_hi_set, 1)
                        dve.wait_ge(max_hi_set, b.count(1, 1))
                        nc.vector.tensor_tensor(max_lo[:], misc_dve[0:H, T:2 * T], max_hi[:], ALU.subtract).then_inc(max_split, 1)
                    b = t.proj
                    if b.live and h == 4:
                        dve.wait_ge(v_mm, b.count(1, 1))
                        if b.later(RING):
                            dve.wait_ge(av_mm, b.count(4, 4 * (1 - RING)))
                        for u in range(2):
                            nc.vector.tensor_tensor(
                                v_aug[b.ring][:, :, u, :, D * u:D * u + D],
                                misc_dve[:, 0:T].rearrange("p (a u g d) -> p a u g d", u=2, g=4, d=D)[:, :, u],
                                bv_sb[:].rearrange("p i (a u g d) -> p (i a) u g d", u=2, g=4, d=D)[:, :, u], ALU.add).then_inc(v_set, 1)
                    b = t.tail
                    if b.live and h == 7:
                        dve.wait_ge(tok_T, b.count(1, 1))
                        v = misc_dve[:].rearrange("p (a w) -> p a w", w=32)
                        nc.vector.reciprocal(recip_sum[:], v[:, :, 2 * D:2 * D + 2]).then_inc(recip_set, 1)
                        dve.wait_ge(recip_set, b.count(1, 1))
                        dve.wait_ge(back_T, b.count(1, 0))
                        nc.vector.tensor_tensor(att_tok[:], v[:, :, 0:2 * D].rearrange("p a (u d) -> p a u d", u=2),
                                                recip_sum[:].unsqueeze(3).to_broadcast([P, 8 * NT, 2, D]), ALU.mult).then_inc(att_norm, 1)
                    if b.live and h == 11:
                        dve.wait_ge(y_mm, b.count(1, 1))
                        dve.wait_ge(xbo_set, b.count(1, 1))
                        nc.vector.tensor_tensor(res[:], misc_dve[:, 0:T].rearrange("p (i c) -> p i c", i=NT), x_bo[:], ALU.add).then_inc(res_set, 1)
                        dve.wait_ge(res_set, b.count(1, 1))
                        for i in range(NT):
                            nc.vector.bn_stats(stats[:, i, :], res[:, i, :]).then_inc(stats_set, 1)
                    if b.live and h == 12:
                        for i in range(NT):
                            nc.vector.bn_aggr(mv[:, i, :], stats[:, i, :]).then_inc(mv_set, 1)
                        dve.wait_ge(mv_set, b.count(NT, NT))
                        dve.wait_ge(rstd_set, b.count(1, 0))
                        nc.vector.tensor_scalar(var_eps[:], mv[:, :, 1], EPS, None, ALU.add).then_inc(eps_set, 1)
                    if b.live and h == 13:
                        dve.wait_ge(rstd_set, b.count(1, 1))
                        dve.wait_ge(x1_T, b.count(1, 0))
                        dve.wait_ge(x1_kept, b.count(1, 0))
                        for i in range(NT):
                            nc.vector.tensor_scalar(x1_new[:, i, :], res[:, i, :], mv[:, i, 0:1], rstd[:, i:i + 1],
                                                    ALU.subtract, ALU.mult).then_inc(x1_set, 1)
                    if b.live and h == 15:
                        dve.wait_ge(gate_mm, b.count(1, 1))
                        nc.vector.tensor_copy(logits[:, bass.ds(b.n * NT, NT), :],
                                              misc_dve[:, T:T + NT * E].rearrange("p (i e) -> p i e", i=NT)).then_inc(logits_set, 1)

            slots(dve, slot)

            full = [P, TILES, E]
            step = [0]

            def route(ins):
                step[0] += 1
                ins.then_inc(route_step, 1)
                dve.wait_ge(route_step, step[0])

            dve.wait_ge(c_in, 16 * 8)
            dve.wait_ge(scores_set, 1)
            route(nc.vector.tensor_tensor(biased[:], scores[:], ebias_sb[:].unsqueeze(1).to_broadcast(full), ALU.add))
            for k, sel in enumerate((first_sel, equal)):
                route(nc.vector.tensor_reduce(best[:], biased[:], AX_X, ALU.max))
                route(nc.vector.tensor_tensor(equal[:], biased[:], best[:].unsqueeze(2).to_broadcast(full), ALU.is_equal))
                route(nc.vector.tensor_tensor(equal[:], equal[:], rank_sb[:].unsqueeze(1).to_broadcast(full), ALU.mult))
                route(nc.vector.tensor_reduce(best[:], equal[:], AX_X, ALU.max))
                route(nc.vector.tensor_tensor(sel[:], equal[:], best[:].unsqueeze(2).to_broadcast(full), ALU.is_equal))
                if k == 0:
                    route(nc.vector.scalar_tensor_tensor(biased[:], first_sel[:], -3.0e38, biased[:], ALU.mult, ALU.add))
            route(nc.vector.tensor_tensor(equal[:], equal[:], first_sel[:], ALU.add))
            nc.vector.tensor_tensor(weights[:], equal[:], scores[:], ALU.mult).then_inc(route_step, 1)
            dve.wait_ge(weights_T, 1)
            nc.vector.tensor_copy(weightsT[:], outT_ps[:].rearrange("p (c t) -> p c t", t=P)).then_inc(weightsT_set, 1)
            dve.wait_ge(x1T_kept, B)
            dve.wait_ge(x1_kept, B)

            def scale_in(g, e):
                n = e + 1
                if past(g, 1) or n > DEPTH:
                    dve.wait_ge(up_mm, g * (2 * NE) + 2 * (n - DEPTH + 1))
                dve.wait_ge(weight_in[e % SB_RING], g * (16 * E // SB_RING) + 16 * (e // SB_RING + 1))
                nc.vector.tensor_tensor(xs[n % DEPTH][:], x1T[:, bass.ds(g * G, G)],
                                        weight_b[e % SB_RING], ALU.mult).then_inc(xs_set, 1)

            def stats_of(g):
                dve.wait_ge(out_T, g)
                nc.vector.tensor_tensor(res2[:], outT_ps[:].rearrange("p (i c) -> p i c", i=GT), x1[:, bass.ds(g * GT - GT, GT), :],
                                        ALU.add).then_inc(res2_set, 1)
                dve.wait_ge(res2_set, g)
                for i in range(GT):
                    nc.vector.bn_stats(stats2[:, i, :], res2[:, i, :]).then_inc(stats2_set, 1)

            def aggregate(g):
                for i in range(GT):
                    nc.vector.bn_aggr(mv2[:, i, :], stats2[:, i, :]).then_inc(mv2_set, 1)
                dve.wait_ge(mv2_set, g * GT)
                if past(g, 2):
                    dve.wait_ge(rstd2_set, g - 1)
                nc.vector.tensor_scalar(var_eps2[:], mv2[:, :, 1], EPS, None, ALU.add).then_inc(eps2_set, 1)

            def norm(g):
                dve.wait_ge(rstd2_set, g)
                if past(g, 2):
                    dve.wait_ge(y_out, g * 16 - 16)
                for i in range(GT):
                    nc.vector.tensor_scalar(y_sb[:, i, :], res2[:, i, :], mv2[:, i, 0:1], rstd2[:, i:i + 1],
                                            ALU.subtract, ALU.mult).then_inc(y_set, 1)

            def group(g):
                scale_in(g, 0)
                for n in range(NE):
                    if past(g, 1) and n == 4:
                        dve.wait_ge(stats2_set, g * GT)
                    if n + 1 < E:
                        scale_in(g, n + 1)
                    if past(g, 1) and n == 4:
                        aggregate(g)
                    dve.wait_ge(act_set, g * NE + (n + 1))
                    dve.wait_ge(up_mm, g * (2 * NE) + (2 * n + 2))
                    if n == DEPTH:
                        dve.wait_ge(down_mm, g * NE + 1)
                    elif n > DEPTH or past(g, 1):
                        dve.wait_ge(hids_set, g * E + (n - DEPTH if n > DEPTH else n - DEPTH + 1))
                    nc.vector.tensor_tensor(hid[n % DEPTH][:], up3_ps[n % DEPTH][:], act[n % DEPTH][:], ALU.mult).then_inc(hid_set, 1)
                    if past(g, 1) and n == 3:
                        stats_of(g)
                    if past(g, 1) and n == 5:
                        norm(g)

            groups(dve, group)
            stats_of(GROUPS)
            dve.wait_ge(stats2_set, GROUPS * GT)
            aggregate(GROUPS)
            norm(GROUPS)


_OUT_SHAPE = (32, 256, 128)


def kernel(**inputs):
    import concourse.bacc as bacc
    from concourse.bass_utils import run_bass_kernel_spmd

    a = {n: np.asarray(v) for n, v in inputs.items()}
    x = a["L0_attn_x"]
    C = x.shape[-1]
    D, P_ = 8, 128
    H = C // D
    E = a["L0_ffn_gate_w"].shape[0]
    wqkv = a["L0_attn_W_qkv"].reshape(H, 3, D, C)
    bqkv = a["L0_attn_b_qkv"].reshape(H, 3, D)
    wo = a["L0_attn_W_out"].T.reshape(2, 2, 4, D, C).transpose(0, 2, 1, 3, 4).reshape(C, C)
    bv = bqkv[:, 2].reshape(1, 1, C)

    def experts(name, shared):
        w = np.concatenate([a[shared][None], a[name]], 0)
        return w.transpose(2, 0, 1)

    arrays = {
        "x": x.reshape(-1, P_, C),
        "xT": x.reshape(-1, C).T,
        "wqT": wqkv[:, 0].reshape(C, C).T,
        "wkT": wqkv[:, 1].reshape(C, C).T,
        "wvT": wqkv[:, 2].reshape(C, C).T,
        "bq": bqkv[:, 0].reshape(C, 1),
        "bk": bqkv[:, 1].reshape(C, 1),
        "bv": np.concatenate([bv, bv], 1),
        "woT": wo,
        "bo": a["L0_attn_b_out"].reshape(1, C),
        "gateT": a["L0_ffn_gate_w"].T,
        "ebias": a["L0_ffn_expert_bias"].reshape(1, E),
        "rank": np.arange(E, 0, -1, dtype=np.float32).reshape(1, E),
        "w1T": experts("L0_ffn_w1", "L0_ffn_sw1"),
        "w3T": experts("L0_ffn_w3", "L0_ffn_sw3"),
        "w2T": experts("L0_ffn_w2", "L0_ffn_sw2"),
    }
    arrays = {n: np.ascontiguousarray(v) for n, v in arrays.items()}
    nc = bacc.Bacc("TRN2", target_bir_lowering=False, num_devices=1)
    args = [nc.dram_tensor(n, v.shape, mybir.dt.from_np(v.dtype), kind="ExternalInput").ap() for n, v in arrays.items()]
    out = nc.dram_tensor("out", (x.size // C // P_, P_, C), F32, kind="ExternalOutput").ap()
    attention_moe_layer(nc, *args, out)
    r = run_bass_kernel_spmd(nc, [arrays], core_ids=[0])
    return r.results[0]["out"].reshape(_OUT_SHAPE)
```

```python
from contextlib import ExitStack

import numpy as np

import concourse.bass as bass
from concourse import mybir

ALU = mybir.AluOpType
ACT = mybir.ActivationFunctionType
AX_X = mybir.AxisListType.X
F32 = mybir.dt.float32
BF16 = mybir.dt.bfloat16
F32R = mybir.dt.float32r

P = 128
RING = 4
PARTS = 3
QPART = (0, 0, 0, 1, 1, 2)
KPART = (0, 1, 2, 0, 1, 0)
TWO_ONES = float(np.array([0x3F803F80], np.uint32).view(np.float32)[0])
MAXROW = 96


class Batch:

    def __init__(self, i, c, batches):
        self.i, self.c = i, c
        self.n = i * RING + c
        self.ring = c % RING
        self.looped = not isinstance(i, int)
        self.live = self.looped or 0 <= c < batches

    def later(self, k):
        assert not self.looped or self.c >= k
        return self.c >= k

    def count(self, per, more):
        assert per * self.c + more >= 0
        return self.i * (RING * per) + (per * self.c + more)

    def lap(self, per, more):
        return self.i * per + (per * (self.c // RING) + more)


def attention_moe_layer(nc, x, xT, wqT, wkT, wvT, bq, bk, bv, woT, bo, gateT, ebias, rank, w1T, w3T, w2T, out):
    C, N = xT.shape
    B = 32
    T = N // B
    NT = T // P
    D = 8
    H = C // D
    E = gateT.shape[1]
    NE = E + 1
    TILES = N // P
    SCALE = float(D) ** -0.5
    EPS = 1e-5
    G = 512
    GT = G // P
    GROUPS = N // G
    NC = len(QPART)
    assert C == P and H == 16 and NT == 2 and NC * D <= MAXROW

    with ExitStack() as ctx:
        def sb(name, shape, dt=F32):
            return ctx.enter_context(nc.sbuf_tensor(name, shape, dt))

        def sem(name):
            return ctx.enter_context(nc.semaphore(name))

        q_parts_dram = nc.dram_tensor("q_parts_dram", [RING, H, NC, D, T], BF16, kind="Internal").ap()
        k_parts_dram = nc.dram_tensor("k_parts_dram", [RING, H, PARTS, D, T], BF16, kind="Internal").ap()
        x1_dram = nc.dram_tensor("x1_dram", [TILES, P, C], F32, kind="Internal").ap()
        route_dram = nc.dram_tensor("route_dram", [TILES, E, P], F32, kind="Internal").ap()

        wq_sb, wk_sb, wv_sb, wo_sb = (sb(n, [P, C]) for n in ("wq_sb", "wk_sb", "wv_sb", "wo_sb"))
        bq_sb, bk_sb, bqs = sb("bq_sb", [P, 1]), sb("bk_sb", [P, 1]), sb("bqs", [P, 1])
        bv_sb = sb("bv_sb", [P, NT, C])
        bo_sb = sb("bo_sb", [P, C])
        gate_sb = sb("gate_sb", [P, E])
        ebias_sb, rank_sb = sb("ebias_sb", [P, E]), sb("rank_sb", [P, E])
        w_hi, w_lo = ([sb(f"{part}_{n}", [P, NE, P], F32R) for n in ("w1", "w3", "w2")] for part in ("hi", "lo"))
        ident = sb("ident", [P, P])
        minus_half = sb("minus_half", [P, GT])
        x1T = sb("x1T", [P, N])
        logits = sb("logits", [P, TILES, E])

        xT_sb = [sb(f"xT_sb{r}", [P, T]) for r in range(RING)]
        x_sb = [sb(f"x_sb{r}", [P, NT, C]) for r in range(RING)]
        q_stack = [sb(f"q_stack{r}", [P, H, T], BF16) for r in range(RING)]
        k_stack = [sb(f"k_stack{r}", [P, H, T], BF16) for r in range(RING)]
        v_aug = [sb(f"v_aug{r}", [P, 2 * NT, 2, 4, 32]) for r in range(RING)]
        negmax = [sb(f"negmax{r}", [P, NT, H]) for r in range(2)]
        qf, kf, rq, rk = (sb(n, [P, T]) for n in ("qf", "kf", "rq", "rk"))
        q_parts, k_parts = sb("q_parts", [P, PARTS, T], BF16), sb("k_parts", [P, PARTS, T], BF16)
        max_hi, max_lo = sb("max_hi", [H, T], BF16), sb("max_lo", [H, T], BF16)
        probs = [sb(f"probs{r}", [P, NT, T]) for r in range(8)]
        attT = sb("attT", [P, 2, T])
        recip_sum = sb("recip_sum", [P, 8 * NT, 2])
        att_tok = sb("att_tok", [P, 8 * NT, 2, D])
        attc = sb("attc", [P, T])
        x_bo = sb("x_bo", [P, NT, C])
        res = sb("res", [P, NT, C])
        stats, mv = sb("stats", [P, NT, 6]), sb("mv", [P, NT, 2])
        var_eps, rstd = sb("var_eps", [P, NT]), sb("rstd", [P, NT])
        x1_new, x1T_new = sb("x1_new", [P, NT, C]), sb("x1T_new", [P, T])

        banks = [ctx.enter_context(nc.psum_tensor(f"bank{n}", [P, 512], F32)) for n in range(8)]
        max_ps, score_ps, av_ps = banks[0:3], banks[3:5], banks[5]
        misc_act, misc_dve = banks[6], banks[7]

        w_in, xT_in, x_in = sem("w_in"), [sem(f"xT_in{r}") for r in range(RING)], [sem(f"x_in{r}") for r in range(RING)]
        c_in = sem("c_in")
        q_clear, k_clear, v_clear, consts_set = sem("q_clear"), sem("k_clear"), sem("v_clear"), sem("consts_set")
        bqs_set = sem("bqs_set")
        qk_mm, v_mm = sem("qk_mm"), sem("v_mm")
        qk_f = sem("qk_f")
        split_step, parts_out = sem("split_step"), sem("parts_out")
        stack_in = [sem(f"stack_in{r}") for r in range(RING)]
        max_in = [sem(f"max_in{r}") for r in range(RING)]
        v_set = sem("v_set")
        max_mm, max_red = sem("max_mm"), sem("max_red")
        max_T, max_hi_set, max_split = sem("max_T"), sem("max_hi_set"), sem("max_split")
        score_mm, exp_done = sem("score_mm"), sem("exp_done")
        av_mm, att_sb = sem("av_mm"), sem("att_sb")
        tok_T, recip_set, att_norm = sem("tok_T"), sem("recip_set"), sem("att_norm")
        back_T, attc_set = sem("back_T"), sem("attc_set")
        y_mm, xbo_set, res_set = sem("y_mm"), sem("xbo_set"), sem("res_set")
        stats_set, mv_set, eps_set, rstd_set = sem("stats_set"), sem("mv_set"), sem("eps_set"), sem("rstd_set")
        x1_set, x1_kept, x1_T, x1T_set, x1T_kept = (sem(n) for n in ("x1_set", "x1_kept", "x1_T", "x1T_set", "x1T_kept"))
        gate_mm, logits_set = sem("gate_mm"), sem("logits_set")

        MAX_BANK = [h % 3 for h in range(H - 1)] + [1]
        MAX_BACK = [next(d for d in range(1, H) if MAX_BANK[(h - d) % H] == MAX_BANK[h]) for h in range(H)]

        class Slot:
            def __init__(self, i, s):
                self.load, self.proj, self.stack, self.maxi, self.neg, self.soft, self.tail, self.norm = (
                    Batch(i, s + k, B) for k in (5, 4, 3, 2, 1, 0, -1, -2))

        PE_MAX, PE_V, PE_X1T, PE_TOK, PE_QK, PE_GATE, PE_BACK, PE_Y = 1, 5, 5, 8, 7, 11, 12, 15
        DVE_AGGR, DVE_MAX, DVE_X1, DVE_V, DVE_TOK, DVE_GATE, DVE_RES = 1, 2, 3, 6, 9, 12, 15
        ACT_ATT, ACT_X1T, ACT_Q, ACT_K, ACT_ATTC = 2, 5, 8, 9, 13

        FIRST, LOOPS = 3, (B - 8) // RING

        def slots(engine, body):
            for s in range(-4, FIRST):
                body(Slot(0, s))
            with engine.Fori(0, LOOPS) as i:
                for s in range(FIRST, FIRST + RING):
                    body(Slot(i, s))
            for s in range(FIRST + RING * LOOPS, B + 2):
                body(Slot(0, s))

        DEPTH = 3
        LAG, HID_LAG, LO_LAG, HI_LAG, POOL_LAG = 4, 1, 3, 1, 1
        places = [stack[:].rearrange("p h t -> p (h t)").bitcast(F32)[:, n * G:(n + 1) * G]
                  for stack in q_stack + k_stack for n in range(H * T // 2 // G)]

        def take(count):
            return [places.pop(0) for _ in range(count)]

        gated, act, hid, hid_s = (take(DEPTH) for _ in range(4))
        weight_b, weight2_b = [v[:].rearrange("p j t -> p (j t)") for v in probs], take(E)
        by_tile = [v.rearrange("p (a e) -> p a e", e=E) for v in take(5)]
        scores, biased, equal, weights, first_sel = by_tile
        weightsT, outT, y_sb, res2 = take(4)
        weightsT, y_sb, res2 = (v.rearrange("p (a c) -> p a c", c=P) for v in (weightsT, y_sb, res2))
        x1_sb = [v.rearrange("p (a c) -> p a c", c=P) for v in take(2)]
        w2_whole = v_aug[0][:].rearrange("p j u g c -> p (j u g c)").rearrange("p (n c) -> p n c", c=P)
        x_hi, x_lo = ([sb(f"x_{part}{r}", [P, G], F32R) for r in range(2)] for part in ("hi", "lo"))
        hs_hi, hs_lo = ([sb(f"hs_{part}{r}", [P, G], F32R) for r in range(DEPTH)] for part in ("hi", "lo"))
        w_stage = [x1T[:, m * NE * P:(m + 1) * NE * P].rearrange("p (n c) -> p n c", n=NE) for m in range(3)]
        best = sb("best", [P, TILES])
        stats2, mv2 = sb("stats2", [P, GT, 6]), sb("mv2", [P, GT, 2])
        var_eps2, rstd2 = sb("var_eps2", [P, GT]), sb("rstd2", [P, GT])
        up1_ps, up3_ps, down_ps = banks[0:3], banks[3:6], banks[6:8]
        scores_set, route_step, weights_T, weightsT_set, route_out = (
            sem(n) for n in ("scores_set", "route_step", "weights_T", "weightsT_set", "route_out"))
        weight_in, x1_in = [sem(f"weight_in{e}") for e in range(E)], [sem(f"x1_in{r}") for r in range(2)]
        w2_in, w_hi_set, w_lo_set, x_hi_set, x_lo_set = (sem(n) for n in ("w2_in", "w_hi_set", "w_lo_set", "x_hi_set", "x_lo_set"))
        gated_set, up_mm, act_set, hid_set, square_set, hids_set, down_mm = (
            sem(n) for n in ("gated_set", "up_mm", "act_set", "hid_set", "square_set", "hids_set", "down_mm"))
        hs_hi_set, hs_lo_dve, hs_lo_pool = sem("hs_hi_set"), sem("hs_lo_dve"), sem("hs_lo_pool")
        outT_set, out_T, res2_set, stats2_set, mv2_set, eps2_set, rstd2_set, y_set, y_out = (
            sem(n) for n in ("outT_set", "out_T", "res2_set", "stats2_set", "mv2_set", "eps2_set", "rstd2_set",
                             "y_set", "y_out"))

        def wait_used(engine, g, n):
            if n % NE in WHOLE:
                engine.wait_ge(down_mm, done(g, n))
            else:
                engine.wait_ge(hs_hi_set, split_done(g, n))
                wait_lo(engine, g, n)

        POOL_LO = (8,)
        WHOLE = (0, 2, 4, 6)
        DVE_LO = tuple(n for n in range(NE) if n not in POOL_LO + WHOLE)
        SPLIT = POOL_LO + DVE_LO

        def split_done(g, n):
            n, g = (n, g) if n >= 0 else (n + NE, g - 1)
            return g * len(SPLIT) + sum(m <= n for m in SPLIT)

        def groups(engine, body):
            for g in range(4):
                body(g, g % 2)
            with engine.Fori(0, (GROUPS - 6) // 2) as i:
                body(i * 2 + 4, 0)
                body(i * 2 + 5, 1)
            body(GROUPS - 2, 0)
            body(GROUPS - 1, 1)

        DRAIN_AT, TOKENS_AT, STATS_AT, MEAN_AT, POW_AT, NORM_AT, HI_AT, LO_AT = 3, 5, 6, 7, 8, 1, 3, 4

        def behind(g, n, lag):
            return None if isinstance(g, int) and (g == 0 and n < lag or g == GROUPS and n >= lag) else n - lag

        def done(g, n):
            return g * NE + (n + 1)

        def routed(g, n):
            return g * E + (n if n >= 0 else n + 1)

        def wait_lo(engine, g, n):
            n, g = (n, g) if n >= 0 else (n + NE, g - 1)
            for by, semaphore in ((DVE_LO, hs_lo_dve), (POOL_LO, hs_lo_pool)):
                if n in by:
                    engine.wait_ge(semaphore, g * len(by) + (by.index(n) + 1))

        def past(g, n):
            return not isinstance(g, int) or g >= n

        block = ctx.enter_context(nc.Block())

        @block.sync
        def _(sp):
            for dst, src in ((wv_sb, wvT), (wq_sb, wqT), (wk_sb, wkT), (bq_sb, bq), (bk_sb, bk),
                             (bv_sb, bv.to_broadcast([P, NT, C]))):
                sp.dma_start(dst[:], src).then_inc(w_in, 16)

            def load(b):
                sp.dma_start(xT_sb[b.ring][:], xT[:, bass.ds(b.n * T, T)]).then_inc(xT_in[b.ring], 16)

            load(Batch(0, 0, B))

            def slot(t):
                b = t.stack
                if b.live and b.later(RING):
                    sp.wait_ge(score_mm, b.count(H, H * (1 - RING)))
                elif b.live:
                    sp.wait_ge(q_clear, b.c + 1)
                    sp.wait_ge(k_clear, 2 * (b.c + 1))
                b = t.load
                if b.live:
                    if b.later(RING) and not t.stack.later(RING):
                        sp.wait_ge(v_mm, b.count(1, 1 - RING))
                    load(b)
                b = t.stack
                if b.live:
                    sp.wait_ge(parts_out, b.count(144, 144))
                    sp.dma_start(q_stack[b.ring][0:NC * D, :, :], q_parts_dram[b.ring].rearrange("h c d t -> (c d) h t")).then_inc(stack_in[b.ring], 16)
                    for row, parts in ((0, 3), (3, 2), (5, 1)):
                        sp.dma_start(k_stack[b.ring][row * D:(row + parts) * D, :, :],
                                     k_parts_dram[b.ring, :, 0:parts].rearrange("h c d t -> (c d) h t")).then_inc(stack_in[b.ring], 16)
                b = t.neg
                if b.live:
                    sp.wait_ge(max_split, b.count(1, 1))
                    for row, part in enumerate((max_hi, max_lo)):
                        sp.dma_start(q_stack[b.ring][MAXROW + row:MAXROW + row + 1, :, :], part[:]).then_inc(max_in[b.ring], 16)
                    if b.later(RING):
                        sp.wait_ge(xbo_set, b.count(1, 1 - RING))
                    sp.dma_start(x_sb[b.ring][:], x[bass.ds(b.n * NT, NT), :, :].rearrange("i p c -> p i c")).then_inc(x_in[b.ring], 16)
                b = t.norm
                if b.live:
                    sp.wait_ge(x1_set, b.count(2, 2))
                    sp.dma_start(x1_dram[bass.ds(b.n * NT, NT), :, :].rearrange("i p c -> p i c"), x1_new[:]).then_inc(x1_kept, 16)
                b = t.proj
                if b.live:
                    sp.wait_ge(split_step, b.count(6, 6))
                    for c, part in enumerate(QPART):
                        sp.dma_start(q_parts_dram[b.ring, :, c], q_parts[:, part, :]).then_inc(parts_out, 16)
                    for c in range(PARTS):
                        sp.dma_start(k_parts_dram[b.ring, :, c], k_parts[:, c, :]).then_inc(parts_out, 16)

            slots(sp, slot)

            sp.wait_ge(weightsT_set, 1)
            sp.dma_start(route_dram.rearrange("(c r) e t -> (r e) c t", r=16), weightsT[:]).then_inc(route_out, 16)
            sp.wait_ge(route_out, 16)

            def write_out(g):
                sp.wait_ge(y_set, g * GT)
                sp.dma_start(out[bass.ds(g * GT - GT, GT), :, :].rearrange("i p c -> p i c"), y_sb[:]).then_inc(y_out, 16)

            sp.wait_ge(x1_kept, 16 * B)

            def group(g, r):
                for e in range(E):
                    n = e + 1
                    if past(g, 1):
                        sp.wait_ge(gated_set, g * E + (e - E + 1))
                        sp.wait_ge(square_set, g * E + (e - E + 1))
                    sp.dma_start(weight_b[e].rearrange("p (a t) -> p a t", t=P),
                                 route_dram[bass.ds(g * GT, GT), e:e + 1, :].rearrange("a e t -> e a t").to_broadcast([P, GT, P])
                                 ).then_inc(weight_in[e], 16)
                    if e == 4:
                        if past(g, 2):
                            sp.wait_ge(res2_set, g - 1)
                        sp.dma_start(x1_sb[r][:], x1_dram[bass.ds(g * GT, GT), :, :].rearrange("i p c -> p i c")).then_inc(x1_in[r], 16)
                    if e == 3 and past(g, 2):
                        write_out(g - 1)

            groups(sp, group)
            write_out(GROUPS - 1)
            write_out(GROUPS)
            sp.wait_ge(y_out, 16 * GROUPS)

        @block.gpsimd
        def _(pool):
            pool.memset(ident[:], 0.0).then_inc(consts_set, 1)
            pool.wait_ge(consts_set, 1)
            pool.affine_select(out=ident[:], in_=ident[:], compare_op=ALU.not_equal, fill=1.0, base=0,
                               pattern=[[-1, P]], channel_multiplier=1).then_inc(consts_set, 1)
            pool.memset(minus_half[:], -0.5).then_inc(consts_set, 1)
            for r in range(RING):
                pool.memset(q_stack[r][:].rearrange("p h t -> p (h t)").bitcast(F32), 0.0).then_inc(q_clear, 1)
            pool.wait_ge(c_in, 16 * 8)

            def slot(t):
                b = t.norm
                if b.live:
                    pool.wait_ge(eps_set, b.count(1, 1))
                    pool.tensor_tensor(rstd[:], var_eps[:], minus_half[:, 0:NT], ALU.pow).then_inc(rstd_set, 1)
                b = t.tail
                if b.live:
                    pool.wait_ge(x_in[b.ring], b.lap(16, 16))
                    if b.later(1):
                        pool.wait_ge(res_set, b.count(1, 0))
                    pool.tensor_tensor(x_bo[:], x_sb[b.ring][:], bo_sb[:].unsqueeze(1).to_broadcast([P, NT, C]), ALU.add).then_inc(xbo_set, 1)
                b = t.norm
                if b.live:
                    pool.wait_ge(x1T_set, b.count(1, 1))
                    pool.tensor_copy(x1T[:, bass.ds(b.n * T, T)], x1T_new[:]).then_inc(x1T_kept, 1)
                b = t.proj
                if b.live:
                    pool.wait_ge(qk_f, b.count(4, 4))
                    for full, rest, parts in ((qf, rq, q_parts), (kf, rk, k_parts)):
                        pool.tensor_tensor(rest[:], full[:], parts[:, 0, :], ALU.subtract).then_inc(split_step, 1)
                        pool.tensor_tensor(parts[:, 1, :], full[:], parts[:, 0, :], ALU.subtract).then_inc(split_step, 1)
                    pool.wait_ge(split_step, b.count(6, 2))
                    pool.tensor_tensor(q_parts[:, 2, :], rq[:], q_parts[:, 1, :], ALU.subtract).then_inc(split_step, 1)
                    pool.wait_ge(split_step, b.count(6, 4))
                    pool.tensor_tensor(k_parts[:, 2, :], rk[:], k_parts[:, 1, :], ALU.subtract).then_inc(split_step, 1)

                    if b.c == RING and not b.looped:
                        for m in range(3):
                            pool.wait_ge(w_hi_set, m + 1)
                            pool.tensor_tensor(w_lo[m][:], w_stage[m], w_hi[m][:], ALU.subtract).then_inc(w_lo_set, 1)

            slots(pool, slot)

            def split_x(g, r):
                pool.wait_ge(x_hi_set, g + 1)
                pool.tensor_tensor(x_lo[r][:], x1T[:, bass.ds(g * G, G)], x_hi[r][:], ALU.subtract).then_inc(x_lo_set, 1)

            def low_part(g, n):
                pool.wait_ge(hs_hi_set, split_done(g, n))
                n, g = (n, g) if n >= 0 else (n + NE, g - 1)
                pool.tensor_tensor(hs_lo[n % DEPTH][:], (hid_s if n else hid)[n % DEPTH], hs_hi[n % DEPTH][:], ALU.subtract).then_inc(hs_lo_pool, 1)

            split_x(0, 0)

            def group(g, r):
                for n in range(NE):
                    if n:
                        if past(g, 1) or n > DEPTH:
                            wait_used(pool, g, n - DEPTH)
                        pool.wait_ge(hid_set, done(g, n))
                        pool.wait_ge(square_set, g * E + n)
                        pool.tensor_tensor(hid_s[n % DEPTH], hid[n % DEPTH], weight2_b[n - 1],
                                           ALU.mult).then_inc(hids_set, 1)
                    m = behind(g, n, POOL_LAG)
                    if m is not None and m % NE in POOL_LO:
                        low_part(g, m)
                    if n == LO_AT and (not isinstance(g, int) or g < GROUPS - 1):
                        split_x(g + 1, 1 - r)
                    if n == POW_AT and past(g, 1):
                        pool.wait_ge(eps2_set, g)
                        pool.tensor_tensor(rstd2[:], var_eps2[:], minus_half[:], ALU.pow).then_inc(rstd2_set, 1)

            groups(pool, group)
            for n in range(POOL_LAG):
                if (n - POOL_LAG) % NE in POOL_LO:
                    low_part(GROUPS, n - POOL_LAG)
            pool.wait_ge(eps2_set, GROUPS)
            pool.tensor_tensor(rstd2[:], var_eps2[:], minus_half[:], ALU.pow).then_inc(rstd2_set, 1)

        @block.scalar
        def _(act_e):
            for dst, src in ((wo_sb, woT), (bo_sb, bo.to_broadcast([P, C])),
                             (gate_sb, gateT), (ebias_sb, ebias.to_broadcast([P, E])), (rank_sb, rank.to_broadcast([P, E])),
                             (w_stage[0], w1T), (w_stage[1], w3T), (w_stage[2], w2T)):
                act_e.dma_start(dst[:], src).then_inc(c_in, 16)

            def slot(t):
                for h in range(H):
                    b = t.soft
                    if b.live:
                        act_e.wait_ge(score_mm, b.count(H, h + 1))
                        if h % 4 == 0 and b.later(1) or h >= 8 and h % 4 == 0:
                            act_e.wait_ge(av_mm, b.count(4, h // 4 - 1))
                        nc.scalar.activation(probs[h % 8][:], score_ps[h % 2][:].rearrange("p (j t) -> p j t", j=NT), ACT.Exp).then_inc(exp_done, 1)
                    b = t.tail
                    if b.live and h == ACT_ATT:
                        act_e.wait_ge(av_mm, b.count(4, 4))
                        if b.later(1):
                            act_e.wait_ge(tok_T, b.count(1, 0))
                        nc.scalar.activation(attT[:], av_ps[:].rearrange("p (a t) -> p a t", a=2), ACT.Copy).then_inc(att_sb, 1)
                    if b.live and h == ACT_ATTC:
                        act_e.wait_ge(back_T, b.count(1, 1))
                        if b.later(1):
                            act_e.wait_ge(y_mm, b.count(1, 0))
                        nc.scalar.activation(attc[:], misc_act[:, 0:T], ACT.Copy).then_inc(attc_set, 1)
                    b = t.norm
                    if b.live and h == ACT_X1T:
                        act_e.wait_ge(x1_T, b.count(1, 1))
                        if b.later(1):
                            act_e.wait_ge(gate_mm, b.count(1, 0))
                            act_e.wait_ge(x1T_kept, b.count(1, 0))
                        nc.scalar.activation(x1T_new[:], misc_act[:, 0:T], ACT.Copy).then_inc(x1T_set, 1)
                    b = t.proj
                    if b.live and h == ACT_Q:
                        if b.c == 0 and not b.looped:
                            act_e.wait_ge(bqs_set, 1)
                        act_e.wait_ge(qk_mm, b.count(1, 1))
                        if b.later(1):
                            act_e.wait_ge(split_step, b.count(6, 0))
                            act_e.wait_ge(parts_out, b.count(144, 0))
                        nc.scalar.activation(qf[:], misc_act[:, 0:T], ACT.Identity, bias=bqs[:, 0:1], scale=SCALE).then_inc(qk_f, 1)
                        nc.scalar.activation(q_parts[:, 0, :], misc_act[:, 0:T], ACT.Identity, bias=bqs[:, 0:1], scale=SCALE).then_inc(qk_f, 1)
                    if b.live and h == ACT_K:
                        nc.scalar.activation(kf[:], misc_act[:, T:2 * T], ACT.Identity, bias=bk_sb[:, 0:1]).then_inc(qk_f, 1)
                        nc.scalar.activation(k_parts[:, 0, :], misc_act[:, T:2 * T], ACT.Identity, bias=bk_sb[:, 0:1]).then_inc(qk_f, 1)

                    if b.live and h == 12 and b.c == RING and not b.looped:
                        act_e.wait_ge(c_in, 16 * 8)
                        for m in range(3):
                            nc.scalar.activation(w_hi[m][:], w_stage[m], ACT.Copy).then_inc(w_hi_set, 1)

            slots(act_e, slot)

            act_e.wait_ge(logits_set, B)
            nc.scalar.activation(scores[:], logits[:], ACT.Sigmoid).then_inc(scores_set, 1)

            def drain(g, r):
                act_e.wait_ge(down_mm, g * NE)
                if past(g, 2):
                    act_e.wait_ge(out_T, g - 1)
                nc.scalar.activation(outT[:], down_ps[r][:], ACT.Copy).then_inc(outT_set, 1)

            def split_x(g, r):
                if not isinstance(g, int) or g:
                    act_e.wait_ge(up_mm, (g - 1) * (2 * NE))
                nc.scalar.activation(x_hi[r][:], x1T[:, bass.ds(g * G, G)], ACT.Copy).then_inc(x_hi_set, 1)

            def square(g, e):
                act_e.wait_ge(weight_in[e], g * 16 + 16)
                if past(g, 1):
                    act_e.wait_ge(hids_set, g * E + (e - E + 1))
                nc.scalar.activation(weight2_b[e], weight_b[e], ACT.Square).then_inc(square_set, 1)

            def high_part(g, n):
                if n % NE:
                    act_e.wait_ge(hids_set, routed(g, n))
                else:
                    act_e.wait_ge(hid_set, done(g, n))
                if past(g, 1) or n >= DEPTH:
                    act_e.wait_ge(down_mm, done(g, n - DEPTH))
                nc.scalar.activation(hs_hi[n % DEPTH][:], (hid_s if n % NE else hid)[n % DEPTH], ACT.Copy).then_inc(hs_hi_set, 1)

            act_e.wait_ge(x1T_kept, B)
            split_x(0, 0)
            act_e.wait_ge(av_mm, 4 * B)
            act_e.dma_start(w2_whole, w2T[:, 0:w2_whole.shape[1]]).then_inc(w2_in, 16)

            def group(g, r):
                for n in range(NE):
                    if n:
                        act_e.wait_ge(gated_set, g * E + n)
                    else:
                        act_e.wait_ge(up_mm, g * (2 * NE) + 1)
                    if past(g, 1) or n >= DEPTH:
                        act_e.wait_ge(hid_set, done(g, n - DEPTH))
                    nc.scalar.activation(act[n % DEPTH], gated[n % DEPTH] if n else up1_ps[0][:], ACT.Silu).then_inc(act_set, 1)
                    if n < E:
                        square(g, n)
                    if n == DRAIN_AT and past(g, 1):
                        drain(g, 1 - r)
                    m = behind(g, n, HI_LAG)
                    if m is not None and m % NE in SPLIT:
                        high_part(g, m)
                    if n == HI_AT and (not isinstance(g, int) or g < GROUPS - 1):
                        split_x(g + 1, 1 - r)

            groups(act_e, group)
            for n in range(HI_LAG):
                if (n - HI_LAG) % NE in SPLIT:
                    high_part(GROUPS, n - HI_LAG)
            drain(GROUPS, 1)

        @block.tensor
        def _(pe):
            def row_maxima_scores(b, h):
                if h == 0:
                    pe.wait_ge(stack_in[b.ring], b.lap(64, 64))
                if b.later(1) or h >= MAX_BACK[h]:
                    pe.wait_ge(max_red, b.count(H, h + 1 - MAX_BACK[h]))
                for i in range(NT):
                    mm = pe.matmul(max_ps[MAX_BANK[h]][:, i * T:(i + 1) * T], q_stack[b.ring][0:MAXROW, h, i * P:(i + 1) * P],
                                   k_stack[b.ring][0:MAXROW, h, :], start=True, stop=True)
                mm.then_inc(max_mm, 1)

            def shifted_scores(b, h):
                if h == 0:
                    pe.wait_ge(max_in[b.ring], b.lap(32, 32))
                    if b.c == 0 and not b.looped:
                        pe.wait_ge(c_in, 16 * 8)
                if b.later(1) or h >= 2:
                    pe.wait_ge(exp_done, b.count(H, h - 1))
                for j in range(NT):
                    mm = pe.matmul(score_ps[h % 2][:, j * T:(j + 1) * T], k_stack[b.ring][:, h, j * P:(j + 1) * P],
                                   q_stack[b.ring][:, h, :], start=True, stop=True)
                mm.then_inc(score_mm, 1)

            def values(b, quad, j):
                half, u = quad // 2, quad % 2
                if j == 0:
                    pe.wait_ge(exp_done, b.count(H, 4 * quad + 4))
                if quad == 0 and j == 0:
                    pe.wait_ge(v_set, b.count(2, 2))
                    if b.later(1):
                        pe.wait_ge(att_sb, b.count(1, 0))
                for hh in range(4):
                    mm = pe.matmul(av_ps[32 * hh:32 * hh + 32, half * T:(half + 1) * T], v_aug[b.ring][:, 2 * j + half, u, hh, :],
                                   probs[4 * (quad % 2) + hh][:, j, :], start=(u == 0 and j == 0), stop=(u == 1 and j == 1))
                if j == 1:
                    mm.then_inc(av_mm, 1)

            def slot(t):
                for h in range(H):
                    if t.maxi.live:
                        row_maxima_scores(t.maxi, h)
                    if t.soft.live:
                        shifted_scores(t.soft, h)
                    b = t.neg
                    if b.live and h == PE_MAX:
                        pe.wait_ge(max_red, b.count(H, H))
                        if t.tail.live and t.tail.later(1):
                            pe.wait_ge(res_set, t.tail.count(1, 0))
                        if b.c == 0 and not b.looped:
                            pe.wait_ge(consts_set, 3)
                        for i in range(NT):
                            mm = pe.transpose(misc_dve[0:H, T + i * P:T + (i + 1) * P], negmax[b.ring % 2][:, i, :], ident[:])
                        mm.then_inc(max_T, 1)
                    if t.tail.live and h in (1, 2):
                        values(t.tail, 3, h - 1)
                    if t.soft.live and h >= 5 and (h - 5) % 4 < 2:
                        values(t.soft, (h - 5) // 4, (h - 5) % 4)
                    b = t.stack
                    if b.live and h == PE_V:
                        pe.wait_ge(xT_in[b.ring], b.lap(16, 16))
                        if t.neg.live:
                            pe.wait_ge(max_split, t.neg.count(1, 1))
                        elif b.later(1):
                            pe.wait_ge(v_set, b.count(2, 0))
                        for i in range(NT):
                            mm = pe.matmul(misc_dve[:, i * P:(i + 1) * P], xT_sb[b.ring][:, i * P:(i + 1) * P], wv_sb[:], start=True, stop=True)
                        mm.then_inc(v_mm, 1)
                    b = t.norm
                    if b.live and h == PE_X1T:
                        pe.wait_ge(x1_set, b.count(2, 2))
                        pe.wait_ge(attc_set, b.count(1, 1))
                        for i in range(NT):
                            mm = pe.transpose(misc_act[:, i * P:(i + 1) * P], x1_new[:, i, :], ident[:])
                        mm.then_inc(x1_T, 1)
                    b = t.tail
                    if b.live and h == PE_TOK:
                        pe.wait_ge(att_sb, b.count(1, 1))
                        if t.neg.live:
                            pe.wait_ge(max_split, t.neg.count(1, 1))
                        if t.stack.live:
                            pe.wait_ge(v_set, t.stack.count(2, 2))
                        if t.norm.live:
                            pe.wait_ge(res_set, t.norm.count(1, 1))
                        for i in range(NT):
                            for half in range(2):
                                mm = pe.transpose(misc_dve[:, (2 * i + half) * P:(2 * i + half + 1) * P],
                                                  attT[:, half, i * P:(i + 1) * P], ident[:])
                        mm.then_inc(tok_T, 1)
                    b = t.proj
                    if b.live and h == PE_QK:
                        if b.c == 0 and not b.looped:
                            pe.wait_ge(w_in, 16 * 6)
                        pe.wait_ge(xT_in[b.ring], b.lap(16, 16))
                        if b.later(1):
                            pe.wait_ge(qk_f, b.count(4, 0))
                        if t.tail.live and t.tail.later(1):
                            pe.wait_ge(attc_set, t.tail.count(1, 0))
                        if t.norm.live:
                            pe.wait_ge(x1T_set, t.norm.count(1, 1))
                        pe.matmul(misc_act[:, 0:T], wq_sb[:], xT_sb[b.ring][:], start=True, stop=True)
                        pe.matmul(misc_act[:, T:2 * T], wk_sb[:], xT_sb[b.ring][:], start=True, stop=True).then_inc(qk_mm, 1)
                    b = t.norm
                    if b.live and h == PE_GATE:
                        pe.wait_ge(x1T_set, b.count(1, 1))
                        if t.tail.live:
                            pe.wait_ge(att_norm, t.tail.count(1, 1))
                        pe.wait_ge(res_set, b.count(1, 1))
                        for i in range(NT):
                            mm = pe.matmul(misc_dve[:, i * E:(i + 1) * E], x1T_new[:, i * P:(i + 1) * P], gate_sb[:], start=True, stop=True)
                        mm.then_inc(gate_mm, 1)
                    b = t.tail
                    if b.live and h == PE_BACK:
                        pe.wait_ge(att_norm, b.count(1, 1))
                        if t.proj.live:
                            pe.wait_ge(qk_f, t.proj.count(4, 4))
                        if t.norm.live:
                            pe.wait_ge(x1T_set, t.norm.count(1, 1))
                        for i in range(NT):
                            mm = pe.transpose(misc_act[:, i * P:(i + 1) * P],
                                              att_tok[:, 8 * i:8 * i + 8].rearrange("p a u d -> p (a u d)"), ident[:])
                        mm.then_inc(back_T, 1)
                    if b.live and h == PE_Y:
                        pe.wait_ge(attc_set, b.count(1, 1))
                        pe.wait_ge(att_norm, b.count(1, 1))
                        if t.norm.live:
                            pe.wait_ge(logits_set, t.norm.count(1, 1))
                        for i in range(NT):
                            mm = pe.matmul(misc_dve[:, i * P:(i + 1) * P], attc[:, i * P:(i + 1) * P], wo_sb[:], start=True, stop=True)
                        mm.then_inc(y_mm, 1)

            slots(pe, slot)

            pe.wait_ge(route_step, 14)
            pe.wait_ge(logits_set, B)
            for c in range(TILES // 16):
                mm = pe.transpose(down_ps[1][:, c * P:(c + 1) * P], weights[:, 16 * c:16 * c + 16, :].rearrange("p a e -> p (a e)"), ident[:])
            mm.then_inc(weights_T, 1)
            pe.wait_ge(w_lo_set, 3)
            pe.wait_ge(w2_in, 16)
            pe.wait_ge(max_red, H * B)
            pe.wait_ge(exp_done, H * B)
            pe.wait_ge(att_sb, B)
            pe.wait_ge(x1T_set, B)
            pe.wait_ge(x1T_kept, B)
            pe.wait_ge(weightsT_set, 1)

            def product(ps, m, n, hi, lo, start=True, stop=True):
                pe.matmul(ps[:], w_hi[m][:, n, :], hi[:], start=start, stop=False)
                pe.matmul(ps[:], w_lo[m][:, n, :], hi[:], start=False, stop=False)
                return pe.matmul(ps[:], w_hi[m][:, n, :], lo[:], start=False, stop=stop)

            def up(g, n, r):
                if past(g, 1) or n >= DEPTH:
                    pe.wait_ge(hid_set, done(g, n - DEPTH))
                if n == 0:
                    pe.wait_ge(x_lo_set, g + 1)
                product(up1_ps[n % DEPTH], 0, n, x_hi[r], x_lo[r]).then_inc(up_mm, 1)
                product(up3_ps[n % DEPTH], 1, n, x_hi[r], x_lo[r]).then_inc(up_mm, 1)

            def down(g, n, r):
                if n == 0 and past(g, 2):
                    pe.wait_ge(res2_set, g - 1)
                if n % NE in WHOLE:
                    if n % NE:
                        pe.wait_ge(hids_set, routed(g, n))
                    else:
                        pe.wait_ge(hid_set, done(g, n))
                    n %= NE
                    pe.matmul(down_ps[r][:], w2_whole[:, n, :], (hid_s if n else hid)[n % DEPTH], start=(n == 0), stop=(n == NE - 1)).then_inc(down_mm, 1)
                    return
                wait_lo(pe, g, n)
                n %= NE
                product(down_ps[r], 2, n, hs_hi[n % DEPTH], hs_lo[n % DEPTH], start=(n == 0), stop=(n == NE - 1)).then_inc(down_mm, 1)

            def by_tokens(g, r):
                pe.wait_ge(outT_set, g)
                for i in range(GT):
                    mm = pe.transpose(down_ps[r][:, i * P:(i + 1) * P], outT[:, i * P:(i + 1) * P], ident[:])
                mm.then_inc(out_T, 1)

            def group(g, r):
                for n in range(NE):
                    up(g, n, r)
                    if n >= LAG or past(g, 1):
                        down(g, n - LAG, r if n >= LAG else 1 - r)
                    if n == TOKENS_AT and past(g, 1):
                        by_tokens(g, 1 - r)

            groups(pe, group)
            for n in range(LAG):
                down(GROUPS, n - LAG, 1)
            by_tokens(GROUPS, 1)

        @block.vector
        def _(dve):
            for r in range(RING):
                flat = k_stack[r][:].rearrange("p h t -> p (h t)").bitcast(F32)
                dve.memset(flat, 0.0).then_inc(k_clear, 1)
                dve.wait_ge(k_clear, 2 * r + 1)
                dve.memset(flat[MAXROW:P, :], TWO_ONES).then_inc(k_clear, 1)
                dve.memset(v_aug[r][:], 0.0).then_inc(v_clear, 1)
                dve.wait_ge(v_clear, 2 * r + 1)
                for u in range(2):
                    ins = dve.memset(v_aug[r][:, :, u, :, 2 * D + u:2 * D + u + 1], 1.0)
                ins.then_inc(v_clear, 1)
            dve.wait_ge(w_in, 16 * 6)
            dve.tensor_scalar(bqs[:], bq_sb[:], SCALE, None, ALU.mult).then_inc(bqs_set, 1)
            dve.wait_ge(v_clear, 2 * RING)

            def slot(t):
                for h in range(H):
                    if t.norm.live and h == DVE_AGGR:
                        dve.wait_ge(stats_set, t.norm.count(NT, NT))
                    b = t.maxi
                    if b.live:
                        dve.wait_ge(max_mm, b.count(H, h + 1))
                        if h == 0 and b.later(2):
                            dve.wait_ge(max_T, b.count(1, -1))
                        nc.vector.tensor_reduce(negmax[b.ring % 2][:, :, h], max_ps[MAX_BANK[h]][:].rearrange("p (i s) -> p i s", i=NT),
                                                AX_X, ALU.max, negate=True).then_inc(max_red, 1)
                    b = t.norm
                    if b.live and h == DVE_AGGR:
                        for i in range(NT):
                            nc.vector.bn_aggr(mv[:, i, :], stats[:, i, :]).then_inc(mv_set, 1)
                        dve.wait_ge(mv_set, b.count(NT, NT))
                        if b.later(1):
                            dve.wait_ge(rstd_set, b.count(1, 0))
                        nc.vector.tensor_scalar(var_eps[:], mv[:, :, 1], EPS, None, ALU.add).then_inc(eps_set, 1)
                    if b.live and h == DVE_X1:
                        dve.wait_ge(rstd_set, b.count(1, 1))
                        if b.later(1):
                            dve.wait_ge(x1_T, b.count(1, 0))
                            dve.wait_ge(x1_kept, b.count(16, 0))
                        for i in range(NT):
                            nc.vector.tensor_scalar(x1_new[:, i, :], res[:, i, :], mv[:, i, 0:1], rstd[:, i:i + 1],
                                                    ALU.subtract, ALU.mult).then_inc(x1_set, 1)
                    if b.live and h == DVE_GATE:
                        dve.wait_ge(gate_mm, b.count(1, 1))
                        nc.vector.tensor_copy(logits[:, bass.ds(b.n * NT, NT), :],
                                              misc_dve[:, 0:NT * E].rearrange("p (i e) -> p i e", i=NT)).then_inc(logits_set, 1)
                    b = t.neg
                    if b.live and h == DVE_MAX:
                        dve.wait_ge(max_T, b.count(1, 1))
                        if b.later(1):
                            prev = Batch(b.i, b.c - 1, B)
                            dve.wait_ge(max_in[prev.ring], prev.lap(32, 32))
                        nc.vector.tensor_copy(max_hi[:], misc_dve[0:H, T:2 * T]).then_inc(max_hi_set, 1)
                        dve.wait_ge(max_hi_set, b.count(1, 1))
                        nc.vector.tensor_tensor(max_lo[:], misc_dve[0:H, T:2 * T], max_hi[:], ALU.subtract).then_inc(max_split, 1)
                    b = t.stack
                    if b.live and h == DVE_V:
                        dve.wait_ge(v_mm, b.count(1, 1))
                        if b.later(RING):
                            dve.wait_ge(av_mm, b.count(4, 4 * (1 - RING)))
                        for u in range(2):
                            nc.vector.tensor_tensor(
                                v_aug[b.ring][:, :, u, :, D * u:D * u + D],
                                misc_dve[:, 0:T].rearrange("p (a u g d) -> p a u g d", u=2, g=4, d=D)[:, :, u],
                                bv_sb[:].rearrange("p i (a u g d) -> p (i a) u g d", u=2, g=4, d=D)[:, :, u], ALU.add).then_inc(v_set, 1)
                    b = t.tail
                    if b.live and h == DVE_TOK:
                        dve.wait_ge(tok_T, b.count(1, 1))
                        v = misc_dve[:].rearrange("p (a w) -> p a w", w=32)
                        nc.vector.reciprocal(recip_sum[:], v[:, :, 2 * D:2 * D + 2]).then_inc(recip_set, 1)
                        dve.wait_ge(recip_set, b.count(1, 1))
                        if b.later(1):
                            dve.wait_ge(back_T, b.count(1, 0))
                        nc.vector.tensor_tensor(att_tok[:], v[:, :, 0:2 * D].rearrange("p a (u d) -> p a u d", u=2),
                                                recip_sum[:].unsqueeze(3).to_broadcast([P, 8 * NT, 2, D]), ALU.mult).then_inc(att_norm, 1)
                    if b.live and h == DVE_RES:
                        dve.wait_ge(y_mm, b.count(1, 1))
                        dve.wait_ge(xbo_set, b.count(1, 1))
                        nc.vector.tensor_tensor(res[:], misc_dve[:, 0:T].rearrange("p (i c) -> p i c", i=NT), x_bo[:], ALU.add).then_inc(res_set, 1)
                        dve.wait_ge(res_set, b.count(1, 1))
                        for i in range(NT):
                            nc.vector.bn_stats(stats[:, i, :], res[:, i, :]).then_inc(stats_set, 1)

            slots(dve, slot)

            full = [P, TILES, E]
            step = [0]

            def route(ins):
                step[0] += 1
                ins.then_inc(route_step, 1)
                dve.wait_ge(route_step, step[0])

            dve.wait_ge(c_in, 16 * 8)
            dve.wait_ge(scores_set, 1)
            route(nc.vector.tensor_tensor(biased[:], scores[:], ebias_sb[:].unsqueeze(1).to_broadcast(full), ALU.add))
            for k, sel in enumerate((first_sel, equal)):
                route(nc.vector.tensor_reduce(best[:], biased[:], AX_X, ALU.max))
                route(nc.vector.tensor_tensor(equal[:], biased[:], best[:].unsqueeze(2).to_broadcast(full), ALU.is_equal))
                route(nc.vector.tensor_tensor(equal[:], equal[:], rank_sb[:].unsqueeze(1).to_broadcast(full), ALU.mult))
                route(nc.vector.tensor_reduce(best[:], equal[:], AX_X, ALU.max))
                route(nc.vector.tensor_tensor(sel[:], equal[:], best[:].unsqueeze(2).to_broadcast(full), ALU.is_equal))
                if k == 0:
                    route(nc.vector.scalar_tensor_tensor(biased[:], first_sel[:], -3.0e38, biased[:], ALU.mult, ALU.add))
            route(nc.vector.tensor_tensor(equal[:], equal[:], first_sel[:], ALU.add))
            nc.vector.tensor_tensor(weights[:], equal[:], scores[:], ALU.mult).then_inc(route_step, 1)
            dve.wait_ge(weights_T, 1)
            nc.vector.tensor_copy(weightsT[:], down_ps[1][:].rearrange("p (c t) -> p c t", t=P)).then_inc(weightsT_set, 1)
            dve.wait_ge(x1T_kept, B)

            def weigh(g, n):
                e = n - 1
                dve.wait_ge(up_mm, g * (2 * NE) + (2 * n + 1))
                if past(g, 1) or n > DEPTH:
                    dve.wait_ge(act_set, done(g, n - DEPTH))
                dve.wait_ge(weight_in[e], g * 16 + 16)
                nc.vector.tensor_tensor(gated[n % DEPTH], up1_ps[n % DEPTH][:], weight_b[e], ALU.mult).then_inc(gated_set, 1)

            def hidden(g, n):
                dve.wait_ge(act_set, done(g, n))
                dve.wait_ge(up_mm, g * (2 * NE) + (2 * n + 2))
                if n == DEPTH:
                    wait_used(dve, g, 0)
                elif n > DEPTH or past(g, 1):
                    dve.wait_ge(hids_set, routed(g, n - DEPTH))
                nc.vector.tensor_tensor(hid[n % DEPTH], up3_ps[n % DEPTH][:], act[n % DEPTH], ALU.mult).then_inc(hid_set, 1)

            def low_part(g, n):
                dve.wait_ge(hs_hi_set, split_done(g, n))
                n, g = (n, g) if n >= 0 else (n + NE, g - 1)
                nc.vector.tensor_tensor(hs_lo[n % DEPTH][:], (hid_s if n else hid)[n % DEPTH], hs_hi[n % DEPTH][:],
                                        ALU.subtract).then_inc(hs_lo_dve, 1)

            def stats_of(g, r):
                dve.wait_ge(out_T, g)
                if past(g, 2):
                    dve.wait_ge(y_set, g * GT - GT)
                if isinstance(g, int):
                    dve.wait_ge(x1_in[r], 16 * ((g - 1) // 2 + 1))
                else:
                    dve.wait_ge(x1_in[r], (g - 1 - r) * 8 + 16)
                nc.vector.tensor_tensor(res2[:], down_ps[r][:].rearrange("p (i c) -> p i c", i=GT), x1_sb[r][:], ALU.add).then_inc(res2_set, 1)
                dve.wait_ge(res2_set, g)
                for i in range(GT):
                    nc.vector.bn_stats(stats2[:, i, :], res2[:, i, :]).then_inc(stats2_set, 1)

            def aggregate(g):
                for i in range(GT):
                    nc.vector.bn_aggr(mv2[:, i, :], stats2[:, i, :]).then_inc(mv2_set, 1)
                dve.wait_ge(mv2_set, g * GT)
                if past(g, 2):
                    dve.wait_ge(rstd2_set, g - 1)
                nc.vector.tensor_scalar(var_eps2[:], mv2[:, :, 1], EPS, None, ALU.add).then_inc(eps2_set, 1)

            def norm(g):
                dve.wait_ge(rstd2_set, g)
                if past(g, 2):
                    dve.wait_ge(y_out, g * 16 - 16)
                for i in range(GT):
                    nc.vector.tensor_scalar(y_sb[:, i, :], res2[:, i, :], mv2[:, i, 0:1], rstd2[:, i:i + 1],
                                            ALU.subtract, ALU.mult).then_inc(y_set, 1)

            def delayed(g, n):
                m = behind(g, n, LO_LAG)
                if m is not None and m % NE in DVE_LO:
                    low_part(g, m)
                m = behind(g, n, HID_LAG)
                if m is not None:
                    hidden(g, m)

            def group(g, r):
                for n in range(NE):
                    if n == MEAN_AT and past(g, 1):
                        dve.wait_ge(stats2_set, g * GT)
                    if n:
                        weigh(g, n)
                    if n == MEAN_AT and past(g, 1):
                        aggregate(g)
                    delayed(g, n)
                    if past(g, 1) and n == STATS_AT:
                        stats_of(g, 1 - r)
                    if past(g, 2) and n == NORM_AT:
                        norm(g - 1)

            groups(dve, group)
            for n in range(LO_LAG):
                delayed(GROUPS, n)
            norm(GROUPS - 1)
            stats_of(GROUPS, 1)
            dve.wait_ge(stats2_set, GROUPS * GT)
            aggregate(GROUPS)
            norm(GROUPS)


_OUT_SHAPE = (32, 256, 128)


def kernel(**inputs):
    import concourse.bacc as bacc
    from concourse.bass_utils import run_bass_kernel_spmd

    a = {n: np.asarray(v) for n, v in inputs.items()}
    x = a["L0_attn_x"]
    C = x.shape[-1]
    D, P_ = 8, 128
    H = C // D
    E = a["L0_ffn_gate_w"].shape[0]
    wqkv = a["L0_attn_W_qkv"].reshape(H, 3, D, C)
    bqkv = a["L0_attn_b_qkv"].reshape(H, 3, D)
    wo = a["L0_attn_W_out"].T.reshape(2, 2, 4, D, C).transpose(0, 2, 1, 3, 4).reshape(C, C)
    bv = bqkv[:, 2].reshape(1, 1, C)

    def experts(name, shared):
        w = np.concatenate([a[shared][None], a[name]], 0)
        return w.transpose(2, 0, 1)

    arrays = {
        "x": x.reshape(-1, P_, C),
        "xT": x.reshape(-1, C).T,
        "wqT": wqkv[:, 0].reshape(C, C).T,
        "wkT": wqkv[:, 1].reshape(C, C).T,
        "wvT": wqkv[:, 2].reshape(C, C).T,
        "bq": bqkv[:, 0].reshape(C, 1),
        "bk": bqkv[:, 1].reshape(C, 1),
        "bv": np.concatenate([bv, bv], 1),
        "woT": wo,
        "bo": a["L0_attn_b_out"].reshape(1, C),
        "gateT": a["L0_ffn_gate_w"].T,
        "ebias": a["L0_ffn_expert_bias"].reshape(1, E),
        "rank": np.arange(E, 0, -1, dtype=np.float32).reshape(1, E),
        "w1T": experts("L0_ffn_w1", "L0_ffn_sw1"),
        "w3T": experts("L0_ffn_w3", "L0_ffn_sw3"),
        "w2T": experts("L0_ffn_w2", "L0_ffn_sw2"),
    }
    arrays = {n: np.ascontiguousarray(v) for n, v in arrays.items()}
    nc = bacc.Bacc("TRN2", target_bir_lowering=False, num_devices=1)
    args = [nc.dram_tensor(n, v.shape, mybir.dt.from_np(v.dtype), kind="ExternalInput").ap() for n, v in arrays.items()]
    out = nc.dram_tensor("out", (x.size // C // P_, P_, C), F32, kind="ExternalOutput").ap()
    attention_moe_layer(nc, *args, out)
    r = run_bass_kernel_spmd(nc, [arrays], core_ids=[0])
    return r.results[0]["out"].reshape(_OUT_SHAPE)
```
